# Optimizing a Trainium2 kernel written in Bass

```python
import numpy as np
import jax
import jax.numpy as jnp

def _softmax(x, axis=-1):
    return jax.nn.softmax(x, axis=axis)

def _gelu(x):
    return jax.nn.gelu(x, approximate=True)

def _silu(x):
    return jax.nn.silu(x)

def _sigmoid(x):
    return jax.nn.sigmoid(x)

def _layernorm(x, axis=-1, eps=1e-05):
    m = jnp.mean(x, axis=axis, keepdims=True)
    v = jnp.var(x, axis=axis, keepdims=True)
    return (x - m) / jnp.sqrt(v + eps)

def _scatter_add(tgt, idx, src, axis=0):
    return tgt.at[idx].add(src)

def _segment_sum(src, seg, n):
    return jax.ops.segment_sum(src, seg, n)
kernel_name = 'mk_gnn_preln_d2_gnn_r64_1d84ca'

def setup_inputs(seed: int=0):
    np.random.seed(seed)
    _w = jnp.asarray

    def _rec_inputs():
        import jax
        import jax.numpy as jnp
        _gk = jax.random.key(seed)
        x = -0.0002117 + 1 * jax.random.normal(jax.random.fold_in(_gk, 1), (50000, 256), jnp.float32)
        src = jax.random.randint(jax.random.fold_in(_gk, 2), (12500,), 0, 50000, jnp.int32)
        dst = jax.random.randint(jax.random.fold_in(_gk, 3), (12500,), 0, 50000, jnp.int32)
        _o = jnp.argsort(dst, stable=True)
        src = src[_o]
        dst = dst[_o]
        edge_attr_256 = -6.47781e-05 + 0.999943 * jax.random.normal(jax.random.fold_in(_gk, 12), (12500, 256), jnp.float32)
        edge_weight = jax.random.uniform(jax.random.fold_in(_gk, 13), (12500,), jnp.float32, 0.0, 1)
        edge_weight1 = jax.random.uniform(jax.random.fold_in(_gk, 14), (12500, 1), jnp.float32, 0.0, 0.999998)
        return (x, src, dst, edge_attr_256, edge_weight, edge_weight1)
    x, src, dst, edge_attr_256, edge_weight, edge_weight1 = _rec_inputs()

    def _L0_gnn_setup():
        import jax, jax.numpy as jnp
        import numpy as np
        N_NODES = 100000
        N_EDGES = 50000
        DIM_IN = 256
        DIM_OUT = 256
        key = jax.random.key(seed)
        ks = jax.random.split(key, 8)
        feat_in = jax.random.normal(ks[0], (N_NODES, DIM_IN), dtype=jnp.float32)
        edge_row = jax.random.randint(ks[1], (N_EDGES,), 0, N_NODES, dtype=jnp.int32)
        edge_col = jax.random.randint(ks[2], (N_EDGES,), 0, N_NODES, dtype=jnp.int32)
        edge_val = jax.random.uniform(ks[3], (N_EDGES,), dtype=jnp.float32)
        s1 = 1.0 / np.sqrt(DIM_IN)
        s2 = 1.0 / np.sqrt(DIM_OUT)
        W1 = jax.random.normal(ks[4], (DIM_IN, DIM_OUT), dtype=jnp.float32) * s1
        b1 = jnp.zeros((DIM_OUT,), dtype=jnp.float32)
        W2 = jax.random.normal(ks[5], (DIM_OUT, DIM_OUT), dtype=jnp.float32) * s2
        b2 = jnp.zeros((DIM_OUT,), dtype=jnp.float32)
        eps = jnp.zeros((1,), dtype=jnp.float32)
        offset = jnp.zeros((DIM_OUT,), dtype=jnp.float32)
        scale = jnp.ones((DIM_OUT,), dtype=jnp.float32)
        return {'feat_in': feat_in, 'edge_row': edge_row, 'edge_col': edge_col, 'edge_val': edge_val, 'W1': W1, 'b1': b1, 'W2': W2, 'b2': b2, 'eps': eps, 'offset': offset, 'scale': scale}
    _L0_gnn_all = _L0_gnn_setup()
    _L0_gnn_in = {k: v for k, v in _L0_gnn_all.items() if k in ('W1', 'b1', 'W2', 'b2', 'eps', 'offset', 'scale')}
    del _L0_gnn_all

    def _L1_gnn_setup():
        import jax, jax.numpy as jnp
        import numpy as np
        import math
        N_NODES = 50000
        N_PAIRS = 12500
        NHEADS = 4
        NUM_FEATURES = 256
        HEAD_DIM = NUM_FEATURES // NHEADS
        key = jax.random.key(seed)
        ks = jax.random.split(key, 8)
        x = jax.random.normal(ks[0], (N_NODES, NUM_FEATURES), dtype=jnp.float32)
        w_ij = jax.random.normal(ks[1], (N_PAIRS, NUM_FEATURES), dtype=jnp.float32)
        idx_i = jax.random.randint(ks[2], (N_PAIRS,), 0, N_NODES)
        idx_j = jax.random.randint(ks[3], (N_PAIRS,), 0, N_NODES)
        phi_r_cut = jax.random.uniform(ks[4], (N_PAIRS, 1), dtype=jnp.float32)
        scale = 1.0 / math.sqrt(HEAD_DIM)
        Wq = jax.random.uniform(ks[5], (NHEADS, HEAD_DIM, HEAD_DIM), jnp.float32, -scale, scale)
        Wk = jax.random.uniform(ks[6], (NHEADS, HEAD_DIM, HEAD_DIM), jnp.float32, -scale, scale)
        Wv = jax.random.uniform(ks[7], (NHEADS, HEAD_DIM, HEAD_DIM), jnp.float32, -scale, scale)
        return {'x': x, 'w_ij': w_ij, 'idx_i': idx_i, 'idx_j': idx_j, 'phi_r_cut': phi_r_cut, 'Wq': Wq, 'Wk': Wk, 'Wv': Wv}
    _L1_gnn_all = _L1_gnn_setup()
    _L1_gnn_in = {k: v for k, v in _L1_gnn_all.items() if k in ('Wq', 'Wk', 'Wv')}
    del _L1_gnn_all
    return {'x': x, 'src': src, 'dst': dst, 'edge_attr_256': edge_attr_256, 'edge_weight': edge_weight, 'edge_weight1': edge_weight1, 'L0_gnn_W1': _L0_gnn_in['W1'], 'L0_gnn_b1': _L0_gnn_in['b1'], 'L0_gnn_W2': _L0_gnn_in['W2'], 'L0_gnn_b2': _L0_gnn_in['b2'], 'L0_gnn_eps': _L0_gnn_in['eps'], 'L0_gnn_offset': _L0_gnn_in['offset'], 'L0_gnn_scale': _L0_gnn_in['scale'], 'L1_gnn_Wq': _L1_gnn_in['Wq'], 'L1_gnn_Wk': _L1_gnn_in['Wk'], 'L1_gnn_Wv': _L1_gnn_in['Wv']}

def reference(x, src, dst, edge_attr_256, edge_weight, edge_weight1, L0_gnn_W1, L0_gnn_b1, L0_gnn_W2, L0_gnn_b2, L0_gnn_eps, L0_gnn_offset, L0_gnn_scale, L1_gnn_Wq, L1_gnn_Wk, L1_gnn_Wv):
    import jax
    import jax.numpy as jnp

    def _L0_gnn_ref(feat_in, edge_row, edge_col, edge_val, W1, b1, W2, b2, eps, offset, scale):
        import jax, jax.numpy as jnp
        import numpy as np
        N_NODES = 100000
        N_EDGES = 50000
        DIM_IN = 256
        DIM_OUT = 256
        msg = edge_val[:, None] * feat_in[edge_col]
        aggr = jax.ops.segment_sum(msg, edge_row, num_segments=feat_in.shape[0])
        aggr = aggr + (1.0 + eps) * feat_in
        h = jnp.maximum(aggr @ W1 + b1, 0.0) @ W2 + b2
        h = jnp.maximum(h, 0.0)
        mean = jnp.mean(h, axis=1, keepdims=True)
        var = jnp.var(h, axis=1, keepdims=True) + 1e-10
        return (h - mean) * scale * jax.lax.rsqrt(var) + offset

    def _L1_gnn_ref(x, w_ij, idx_i, idx_j, phi_r_cut, Wq, Wk, Wv):
        import jax, jax.numpy as jnp
        import numpy as np
        import math
        N_NODES = 50000
        N_PAIRS = 12500
        NHEADS = 4
        NUM_FEATURES = 256
        HEAD_DIM = NUM_FEATURES // NHEADS
        n = x.shape[0]
        xh = x.reshape(n, NHEADS, HEAD_DIM)
        wh = w_ij.reshape(-1, NHEADS, HEAD_DIM)
        q = jnp.einsum('nhd,hed->nhe', xh, Wq)
        k = jnp.einsum('nhd,hed->nhe', xh, Wk)
        v = jnp.einsum('nhd,hed->nhe', xh, Wv)
        inv_sqrt_d = 1.0 / math.sqrt(HEAD_DIM)
        alpha = (q[idx_i] * wh * k[idx_j]).sum(axis=-1) * inv_sqrt_d
        alpha = alpha * phi_r_cut
        msg = alpha[:, :, None] * v[idx_j]
        y = jax.ops.segment_sum(msg, idx_i, num_segments=n)
        return y.reshape(n, NHEADS * HEAD_DIM)
    h = jnp.maximum(_layernorm(x, axis=-1), 0.0)
    x = x + _L0_gnn_ref(h, src, dst, edge_weight, L0_gnn_W1, L0_gnn_b1, L0_gnn_W2, L0_gnn_b2, L0_gnn_eps, L0_gnn_offset, L0_gnn_scale)
    h = jnp.maximum(_layernorm(x, axis=-1), 0.0)
    x = x + _L1_gnn_ref(h, edge_attr_256, src, dst, edge_weight1, L1_gnn_Wq, L1_gnn_Wk, L1_gnn_Wv)
    return x

_drawn_inputs = setup_inputs


def setup_inputs(seed=0):
    import zlib

    import numpy as np

    out = dict(_drawn_inputs(seed))
    spreads = {'L0_gnn_b1': (0.0, 0.1),
     'L0_gnn_b2': (0.0, 0.1),
     'L0_gnn_offset': (0.0, 0.1),
     'L0_gnn_scale': (1.0, 0.2)}
    factors = {'edge_attr_256': 3.052,
     'edge_weight1': 6.119,
     'L1_gnn_Wq': 3.208,
     'L1_gnn_Wk': 3.22,
     'L1_gnn_Wv': 3.013}
    for name, (base, spread) in spreads.items():
        noise = np.random.default_rng([zlib.crc32(name.encode()), seed]).standard_normal(out[name].shape)
        drawn = base * np.exp(spread * noise) if base else spread * noise
        out[name] = jnp.asarray(drawn.astype(out[name].dtype))
    for name, factor in factors.items():
        out[name] = (out[name] * factor).astype(out[name].dtype)
    return out
```

```python
from contextlib import ExitStack

import concourse.bass as bass
from concourse import mybir

F32 = mybir.dt.float32
BF16 = mybir.dt.bfloat16
I32 = mybir.dt.int32
ALU = mybir.AluOpType
ACT = mybir.ActivationFunctionType

P = 128
SUB = 4
BLOCK = P * SUB
RADIX = 256
FIELDS = 8
KEY, DST, WEIGHT0, WEIGHT1, EID = range(5)
PAD_KEY = 65535
LN_EPS = 1e-5
POST_EPS = 1e-10


class At:

    def __init__(self, base, it=None, stride=0):
        self.base, self.it, self.stride = base, it, stride

    def back(self, n):
        return At(self.base - n, self.it, self.stride)

    def lin(self, scale, add=0):
        v = self.base * scale + add
        return v if self.it is None else self.it * (self.stride * scale) + v

    @property
    def n(self):
        return self.lin(1)

    def turn(self, ring):
        assert self.it is None or self.stride % ring == 0
        return self.base % ring

    def round(self, ring, scale=1, add=0):
        assert self.it is None or self.stride % ring == 0
        v = (self.base // ring + add) * scale
        return v if self.it is None else self.it * (self.stride // ring * scale) + v


def blocks(eng, first, end, body, unroll=4, peel=0):
    for i in range(first, first + peel):
        body(At(i))
    first += peel
    rounds = (end - first) // unroll
    if rounds >= 2:
        with eng.Fori(0, rounds) as it:
            for u in range(unroll):
                body(At(first + u, it, unroll))
        first += rounds * unroll
    for i in range(first, end):
        body(At(i))


def gnn_kernel(nc, x, src, dst, edge_attr, w0, w1, W1, b1, W2, b2, eps, offset, scale, Wq, Wk, Wv, out):
    N, D = x.shape
    E = src.shape[0]
    H, HD = Wq.shape[0], Wq.shape[1]
    CH = D // P
    T = -(-E // BLOCK) * SUB
    EP = T * P
    EPART = E // T
    assert EPART * T == E and N < PAD_KEY and D == 2 * P and H * HD == D
    DENSE = -(-N // BLOCK)
    EDGE = T // SUB
    ALL = DENSE + EDGE

    hidden = nc.dram_tensor("hidden", (N, D), F32, kind="Internal").ap()
    sorted_by = [nc.dram_tensor(f"sorted_{k}", (EP, FIELDS), I32, kind="Internal").ap() for k in range(2)]

    with ExitStack() as ctx:
        def sb(name, shape, dt=F32):
            return ctx.enter_context(nc.sbuf_tensor(name, shape, dt))

        def ps(name, shape):
            return ctx.enter_context(nc.psum_tensor(name, shape, F32))

        def sem(name):
            return ctx.enter_context(nc.semaphore(name))

        ident = sb("ident", [P, P])
        col_i, col_f = sb("col_i", [P, RADIX], I32), sb("col_f", [P, RADIX])
        row_i, row_f = sb("row_i", [P, 1], I32), sb("row_f", [P, 1])
        ones_f = sb("ones_f", [P, RADIX])
        all_ones, before, not_before = (sb(n, [P, P], BF16) for n in ("all_ones", "before", "not_before"))
        W1_sb, W2_sb = sb("W1_sb", [P, CH, D]), sb("W2_sb", [P, CH, D])
        b1_sb = sb("b1_sb", [P, CH])
        b2_sb, offset_sb, scale_sb = sb("b2_sb", [P, D]), sb("offset_sb", [P, D]), sb("scale_sb", [P, D])
        eps_sb, self_w = sb("eps_sb", [P, 1]), sb("self_w", [P, 1])
        ln_eps, post_eps = sb("ln_eps", [P, 1]), sb("post_eps", [P, 1])
        w_nat = sb("w_nat", [P, 3, CH, P])
        w_qkv = sb("w_qkv", [P, CH, 3, P])

        raw = [sb(f"raw_{n}", [P, T], I32) for n in ("src", "dst", "w0", "w1", "eid")]
        rec = sb("rec", [P, T, FIELDS], I32)
        onehot = sb("onehot", [P, T + 2, RADIX], BF16)
        digit_i, digit_f = sb("digit_i", [P, T], I32), sb("digit_f", [P, T])
        counts, upto, bucket = sb("counts", [P, RADIX]), sb("upto", [P, RADIX]), sb("bucket", [P, RADIX])
        junk = sb("junk", [P, 2, RADIX])
        place_f, place_i, place_lo, place_hi = sb("place_f", [P, T]), sb("place_i", [P, T], I32), sb("place_lo", [P, T], I32), sb("place_hi", [P, T], I32)
        moving = sb("moving", [P, 2, SUB, FIELDS], I32)
        after = sb("after", [P, T, FIELDS], I32)
        prior = sb("prior", [1, T, FIELDS], I32)
        key_f, after_f, same_next = sb("key_f", [P, T]), sb("after_f", [P, T]), sb("same_next", [P, T])
        prior_f, same_prior = sb("prior_f", [1, T]), sb("same_prior", [1, T])
        eid_f, w1_f = sb("eid_f", [P, T]), sb("w1_f", [P, T])
        GATHER_SRC, GATHER_DST, GATHER_EDGE, SCATTER = range(4)
        index = sb("index", [P, 4, T], I32)

        RX, RY = 4, 2
        x_sb = sb("x_sb", [P, RX, SUB, D])
        xo = sb("xo", [P, 4, SUB, D])
        xd = sb("xd", [P, RY, SUB, D])
        bn = sb("bn", [P, 2, SUB, 6])
        mv = sb("mv", [P, RY, 2, SUB, 2])
        std, rstd, shift = (sb(n, [P, RY, 2, SUB]) for n in ("std", "rstd", "shift"))
        h = sb("h", [P, RY, SUB, D])
        h_self = sb("h_self", [P, SUB, D])
        msg = sb("msg", [P, SUB, D])
        key_b = sb("key_b", [P, SUB, P])
        equal = sb("equal", [P, SUB, P])
        hT = sb("hT", [P, RY, CH, BLOCK])
        z1 = sb("z1", [P, RY, CH, BLOCK])
        y = sb("y", [P, RY, SUB, D])
        bn2 = sb("bn2", [P, SUB, 6])
        mv2 = sb("mv2", [P, RY, SUB, 2])
        std2, rstd2 = sb("std2", [P, RY, SUB]), sb("rstd2", [P, RY, SUB])
        fin = sb("fin", [P, RY, SUB, D])
        carry_sb = sb("carry_sb", [1, D])
        idx = sb("idx", [P, 2, 2, SUB], I32)
        idx1 = sb("idx1", [P, 2, 3, SUB], I32)
        prod = sb("prod", [P, 2, D])
        alpha, alpha_w = sb("alpha", [P, 2, H]), sb("alpha_w", [P, 2, H])
        idx_w = sb("idx_w", [P, 2, SUB], I32)

        bank = [ps(f"bank{k}", [P, 512]) for k in range(8)]

        s = {n: sem(n) for n in (
            "const_in", "edges_in", "iota_done", "const_made", "w_filled", "w_turned", "w_ready", "raw_ready",
            "rec_ready", "digit_ready", "onehot_ready", "counted", "bucket_step", "bucket_ready", "rank_a", "rank_b",
            "rank_a_read", "rank_b_read", "place_step", "place_ready", "moved", "scattered_0", "scattered_1",
            "sorted_in", "fields_step", "index_ready",
            "stat_raw", "stat", "std_ready", "rstd_ready", "normed", "xo_made", "turned", "hT_ready",
            "l1_done", "z1_ready", "l2_done", "b2_added", "relu_done", "stat2_raw", "stat2", "std2_ready",
            "rstd2_ready", "scaled", "finished", "idx_ready", "key_spread", "key_turned", "equal_ready",
            "weighted", "carried", "summed", "carry_read", "block_h",
            "x_in0", "x_in1", "x_in2", "x_in3", "stored0", "stored1", "gathered0", "gathered1",
            "scat_idx_ready", "pool_passed", "w_taken", "b_normed", "b_finished", "b_idx_ready", "b_scat_ready", "b_stat_raw", "b_stat", "b_std_ready", "b_rstd_step", "b_rstd_ready", "b_key_spread", "b_key_turned", "b_equal_ready", "b_qkv_done", "b_qw", "b_qwk", "b_alpha", "b_alpha_w", "b_msg", "b_carried", "b_msg_ready", "b_summed", "b_added", "b_turned", "b_turned_taken", "b_gathered0", "b_gathered1", "b_out0", "b_out1",
             "dve_passed", "scat_out0", "scat_out1", "rstd_step", "carry_saved", "msg_ready", "rows_in0", "rows_in1", "rstdB", "xdone",
        )}
        x_in = [s[f"x_in{k}"] for k in range(4)]
        stored = [s["stored0"], s["stored1"]]
        gathered = [s["gathered0"], s["gathered1"]]
        scattered = [s["scattered_0"], s["scattered_1"]]
        scat_out = [s["scat_out0"], s["scat_out1"]]
        b_gathered = [s["b_gathered0"], s["b_gathered1"]]
        b_out = [s["b_out0"], s["b_out1"]]

        block = ctx.enter_context(nc.Block())

        def block_rows(t, a):
            at = a if isinstance(a, int) else a.lin(BLOCK)
            return t[bass.ds(at, BLOCK), :].rearrange("(p j) f -> p j f", j=SUB)

        LAST = N - BLOCK
        DENSE_STORED = 2 * 16 * (DENSE // RY)
        assert DENSE % RY == 0

        def pipeline(eng, step, total, lags, edge_from=None):
            edge_from = total if edge_from is None else edge_from

            def flags(i):
                return {lag: (0 <= i - lag < total, i - lag >= edge_from) for lag in lags}
            first, stop = lags[0], total + lags[-1]
            while first < stop:
                end = first + 1
                while end < stop and flags(end) == flags(first):
                    end += 1
                f = flags(first)

                def body(a, f=f):
                    step(lambda lag: (a.back(lag) if f[lag][0] else None), lambda lag: f[lag][1])
                peel = 4 if first < 8 else 2 if first == edge_from + lags[-1] else 0
                blocks(eng, first, end, body, peel=min(end - first, peel))
                first = end

        LAYER0 = dict(total=ALL, lags=range(-2, 4), edge_from=DENSE)
        LAYER1 = dict(total=EDGE, lags=range(-3, 2))

        @block.sync
        def _(sp):
            with nc.allow_non_contiguous_dma(reason="a column of biases"):
                sp.dma_start(b1_sb[:], b1.rearrange("(c p) -> p c", p=P)).then_inc(s["const_in"], 16)
            for to, of in ((W1_sb, W1), (W2_sb, W2)):
                sp.dma_start(to[:], of.rearrange("(c p) n -> p c n", p=P)).then_inc(s["const_in"], 16)
            for to, of in ((b2_sb, b2), (offset_sb, offset), (scale_sb, scale), (eps_sb, eps)):
                sp.dma_start(to[:], of.partition_broadcast(P)).then_inc(s["const_in"], 16)
            sp.wait_ge(s["raw_ready"], 1)
            for r, of in zip(raw, (src, dst, w0, w1)):
                of = of if len(of.shape) == 1 else of.rearrange("a b -> (a b)")
                of = of if of.dtype == I32 else of.bitcast(I32)
                sp.dma_start(r[0:EPART, :], of.rearrange("(p t) -> p t", t=T)).then_inc(s["edges_in"], 16)
            sp.wait_ge(s["w_filled"], 1)
            for k, W in enumerate((Wq, Wk, Wv)):
                for hh in range(H):
                    c, o = hh // 2, hh % 2 * HD
                    sp.dma_start(w_nat[o:o + HD, k, c, o:o + HD], W[hh]).then_inc(s["w_turned"], 16)
            for k in range(2):
                sp.wait_ge(scattered[0], 16 * SUB * (k + 1) * len(range(0, T // SUB, 2)))
                sp.wait_ge(scattered[1], 16 * SUB * (k + 1) * len(range(1, T // SUB, 2)))
                sp.dma_start(rec[:], sorted_by[k].rearrange("(p t) c -> p t c", t=T)).then_inc(s["sorted_in"], 16)
            sp.wait_ge(s["raw_ready"], 2)
            rows = sorted_by[1]
            sp.dma_start(after[0:P - 1], rows[T:EP].rearrange("(p t) c -> p t c", t=T)).then_inc(s["sorted_in"], 16)
            sp.dma_start(after[P - 1:P, 0:T - 1], rows[1:T].unsqueeze(0)).then_inc(s["sorted_in"], 16)
            sp.dma_start(prior[0:1, 1:T], rows[EP - T:EP - 1].unsqueeze(0)).then_inc(s["sorted_in"], 16)

            def load(a, row=None):
                if a.base >= RX:
                    sp.wait_ge(s["normed"], a.lin(1, 1 - RX))
                    sp.wait_ge(s["xo_made"], a.lin(1, 1 - RX))
                sp.dma_start(x_sb[:, a.turn(RX)], block_rows(x, a if row is None else row)).then_inc(x_in[a.turn(RX)], 16)

            def store(a, row=None):
                sp.wait_ge(s["finished"], a.lin(1, 1))
                for t in (hidden, out):
                    sp.dma_start(block_rows(t, a if row is None else row), fin[:, a.turn(RY)]).then_inc(stored[a.turn(RY)], 16)

            LEAD = 6

            def load_and_store(a):
                store(a.back(LEAD))
                load(a)
            for i in range(LEAD):
                load(At(i))
            blocks(sp, LEAD, DENSE - 1, load_and_store)
            store(At(DENSE - 1 - LEAD))
            load(At(DENSE - 1), row=LAST)
            for i in range(DENSE - LEAD, DENSE - 1):
                store(At(i))
            sp.wait_ge(stored[(DENSE - 2) % RY], DENSE_STORED)
            store(At(DENSE - 1), row=LAST)

        @block.gpsimd
        def _(pool):
            pool.iota(col_i[:], [[1, RADIX]], base=0, channel_multiplier=0).then_inc(s["iota_done"], 1)
            pool.iota(row_i[:], [[0, 1]], base=0, channel_multiplier=1).then_inc(s["iota_done"], 1)
            pool.iota(raw[4][:], [[1, T]], base=0, channel_multiplier=T).then_inc(s["iota_done"], 1)

            for k in range(2):
                pool.wait_ge(s["place_ready"], k + 1)

                def scatter_group(g, k=k):
                    b = g.turn(2)
                    if k or g.base >= 2:
                        done = k * len(range(b, T // SUB, 2))
                        pool.wait_ge(scattered[b], g.round(2, 16 * SUB, done))
                    pool.tensor_copy(moving[:, b], rec[:, bass.ds(g.lin(SUB), SUB), :]).then_inc(s["moved"], 1)
                    pool.wait_ge(s["moved"], g.lin(1, 1 + k * (T // SUB)))
                    pool.sem_inc(s["pool_passed"], 1)
                    for j in range(SUB):
                        pool.indirect_dma_start(
                            sorted_by[k], bass.IndirectOffsetOnAxis(ap=moving[:, b, j, FIELDS - 1:FIELDS], axis=0),
                            moving[:, b, j, :], None).then_inc(scattered[b], 16)
                blocks(pool, 0, T // SUB, scatter_group, unroll=2, peel=2)

            def residual(m, edge):
                if edge:
                    pool.wait_ge(gathered[m.turn(2)], m.back(DENSE).round(2, 16 * 2 * SUB, 1))
                else:
                    pool.wait_ge(x_in[m.turn(RX)], m.round(RX, 16, 1))
                if m.base >= 4:
                    pool.wait_ge(s["finished"], m.lin(1, -3))
                pool.tensor_tensor(xo[:, m.turn(4)], x_sb[:, m.turn(RX)],
                                   offset_sb[:].unsqueeze(1).to_broadcast([P, SUB, D]), ALU.add).then_inc(s["xo_made"], 1)

            def gather(m):
                k, q = m.back(DENSE), m.turn(2)
                pool.wait_ge(s["normed"], m.lin(1, -1))
                pool.wait_ge(s["xo_made"], m.lin(1, 1 - RX))
                pool.tensor_copy(idx[:, q], index[:, 0:2, bass.ds(k.lin(SUB), SUB)]).then_inc(s["idx_ready"], 1)
                pool.wait_ge(s["idx_ready"], k.lin(1, 1))
                pool.sem_inc(s["pool_passed"], 1)
                for j in range(SUB):
                    for side, to in ((GATHER_SRC, x_sb[:, m.turn(RX), j]), (GATHER_DST, xd[:, q, j])):
                        pool.indirect_dma_start(to, None, x, bass.IndirectOffsetOnAxis(
                            ap=idx[:, q, side, j:j + 1], axis=0)).then_inc(gathered[q], 16)

            def scatter(m):
                k, q = m.back(DENSE), m.turn(2)
                if k.base >= 2:
                    pool.wait_ge(scat_out[q], k.round(2, 16 * SUB))
                pool.tensor_copy(idx_w[:, q], index[:, SCATTER, bass.ds(k.lin(SUB), SUB)]).then_inc(s["scat_idx_ready"], 1)
                pool.wait_ge(s["scat_idx_ready"], k.lin(1, 1))
                pool.wait_ge(s["finished"], m.lin(1, 1))
                pool.sem_inc(s["pool_passed"], 1)
                for j in range(SUB):
                    pool.indirect_dma_start(hidden, bass.IndirectOffsetOnAxis(ap=idx_w[:, q, j:j + 1], axis=0),
                                            fin[:, q, j], None, bounds_check=N - 1, oob_is_err=False).then_inc(scat_out[q], 16)

            pool.wait_ge(s["const_in"], 7 * 16)
            pool.wait_ge(s["index_ready"], 1)

            def turn(runs, edge):
                if runs(-2) and edge(-2):
                    gather(runs(-2))
                if runs(0):
                    residual(runs(0), edge(0))
                if runs(3) and edge(3):
                    if runs(3).base == DENSE:
                        pool.wait_ge(stored[0], DENSE_STORED)
                        pool.wait_ge(stored[1], DENSE_STORED)
                    scatter(runs(3))
            pipeline(pool, turn, **LAYER0)

            def gather1(k):
                q, r = k.turn(2), k.turn(RX)
                if k.base >= 2:
                    pool.wait_ge(s["b_normed"], k.lin(1, -1))
                if k.base >= RX:
                    pool.wait_ge(s["b_finished"], k.lin(1, 1 - RX))
                pool.tensor_copy(idx1[:, q], index[:, 0:3, bass.ds(k.lin(SUB), SUB)]).then_inc(s["b_idx_ready"], 1)
                pool.wait_ge(s["b_idx_ready"], k.lin(1, 1))
                pool.sem_inc(s["pool_passed"], 1)
                for j in range(SUB):
                    for side, to, of in ((GATHER_SRC, x_sb[:, r, j], hidden), (GATHER_DST, xd[:, q, j], hidden),
                                         (GATHER_EDGE, xo[:, r, j], edge_attr)):
                        pool.indirect_dma_start(to, None, of, bass.IndirectOffsetOnAxis(
                            ap=idx1[:, q, side, j:j + 1], axis=0)).then_inc(b_gathered[q], 16)

            def scatter1(k):
                q = k.turn(2)
                if k.base >= 2:
                    pool.wait_ge(b_out[q], k.round(2, 16 * SUB))
                pool.tensor_copy(idx_w[:, q], index[:, SCATTER, bass.ds(k.lin(SUB), SUB)]).then_inc(s["b_scat_ready"], 1)
                pool.wait_ge(s["b_scat_ready"], k.lin(1, 1))
                pool.wait_ge(s["b_finished"], k.lin(1, 1))
                pool.sem_inc(s["pool_passed"], 1)
                for j in range(SUB):
                    pool.indirect_dma_start(out, bass.IndirectOffsetOnAxis(ap=idx_w[:, q, j:j + 1], axis=0),
                                            fin[:, q, j], None, bounds_check=N - 1, oob_is_err=False).then_inc(b_out[q], 16)

            for q in range(2):
                pool.wait_ge(scat_out[(DENSE + q) % 2], 16 * SUB * len(range(q, EDGE, 2)))

            def turn1(runs, edge):
                if runs(1):
                    scatter1(runs(1))
                if runs(-3):
                    gather1(runs(-3))
            pipeline(pool, turn1, **LAYER1)
            for q in range(2):
                pool.wait_ge(b_out[q], 16 * SUB * len(range(q, EDGE, 2)))

        @block.vector
        def _(dve):
            for r, v in zip(raw[:4], (PAD_KEY, 0, 0, 0)):
                i = dve.memset(r[:], v)
            dve.memset(rec[:, :, 5:], 0)
            i.then_inc(s["raw_ready"], 1)
            dve.memset(w_nat[:], 0.0).then_inc(s["w_filled"], 1)
            dve.memset(after[:], -1)
            dve.memset(prior[:], -1).then_inc(s["raw_ready"], 1)
            dve.memset(ln_eps[:], LN_EPS)
            dve.memset(post_eps[:], POST_EPS)
            dve.memset(ones_f[:], 1.0)
            dve.memset(all_ones[:], 1.0)
            dve.memset(onehot[:, 0:2, :], 0.0)
            dve.wait_ge(s["iota_done"], 3)
            dve.tensor_copy(col_f[:], col_i[:]).then_inc(s["const_made"], 1)
            dve.tensor_copy(row_f[:], row_i[:]).then_inc(s["const_made"], 1)
            dve.wait_ge(s["const_made"], 2)
            dve.tensor_scalar(ident[:], col_f[:, 0:P], row_f[:, 0:1], None, ALU.is_equal)
            dve.tensor_scalar(before[:], col_f[:, 0:P], row_f[:, 0:1], None, ALU.is_gt)
            dve.tensor_scalar(not_before[:], col_f[:, 0:P], row_f[:, 0:1], None, ALU.is_le).then_inc(s["const_made"], 1)
            dve.wait_ge(s["edges_in"], 4 * 16)
            for c, r in enumerate(raw):
                i = dve.tensor_copy(rec[:, :, c], r[:])
            i.then_inc(s["rec_ready"], 1)
            dve.wait_ge(s["const_in"], 7 * 16)
            dve.tensor_scalar(self_w[:], eps_sb[:], 1.0, None, ALU.add)

            for k in range(2):
                if k:
                    dve.wait_ge(s["sorted_in"], 16)
                else:
                    dve.wait_ge(s["rec_ready"], 1)
                dve.tensor_scalar(digit_i[:], rec[:, :, KEY], 8 * k, RADIX - 1, ALU.logical_shift_right,
                                  ALU.bitwise_and).then_inc(s["digit_ready"], 1)
                dve.wait_ge(s["digit_ready"], 2 * k + 1)
                dve.tensor_copy(digit_f[:], digit_i[:]).then_inc(s["digit_ready"], 1)
                dve.wait_ge(s["digit_ready"], 2 * k + 2)

                def one_hot(t):
                    dve.tensor_scalar(onehot[:, bass.ds(t.lin(1, 2), 1), :].squeeze(1), col_f[:],
                                      digit_f[:, bass.ds(t.n, 1)], None, ALU.is_equal).then_inc(s["onehot_ready"], 1)
                blocks(dve, 0, T, one_hot)

                dve.wait_ge(s["counted"], k + 1)
                dve.tensor_copy(counts[:], bank[2][:, 0:RADIX]).then_inc(s["bucket_step"], 1)
                dve.wait_ge(s["bucket_step"], 2 * k + 1)
                dve.tensor_tensor_scan(upto[:], ones_f[:], counts[:], 0.0, ALU.mult, ALU.add).then_inc(s["bucket_step"], 1)
                dve.wait_ge(s["bucket_step"], 2 * k + 2)
                dve.tensor_tensor(bucket[:], upto[:], counts[:], ALU.subtract).then_inc(s["bucket_ready"], 1)

                def rank_pair(g, k=k):
                    for half, (ready, read) in enumerate((("rank_a", "rank_a_read"), ("rank_b", "rank_b_read"))):
                        dve.wait_ge(s[ready], g.lin(1, 1 + k * (T // 2)))
                        dve.scalar_tensor_tensor(
                            junk[:, half], bank[half][:, 0:RADIX], 1.0, onehot[:, bass.ds(g.lin(2, 2 + half), 1), :].squeeze(1),
                            ALU.mult, ALU.mult, accum_out=place_f[:, bass.ds(g.lin(2, half), 1)]).then_inc(s[read], 1)
                blocks(dve, 0, T // 2, rank_pair, unroll=2)

                dve.wait_ge(s["rank_a_read"], (k + 1) * (T // 2))
                dve.wait_ge(s["rank_b_read"], (k + 1) * (T // 2))
                dve.tensor_copy(place_i[:], place_f[:]).then_inc(s["place_step"], 1)
                dve.wait_ge(s["place_step"], 2 * k + 1)
                dve.tensor_scalar(place_lo[:], place_i[:], P - 1, None, ALU.bitwise_and)
                dve.tensor_scalar(place_hi[:], place_i[:], P.bit_length() - 1, None, ALU.logical_shift_right).then_inc(s["place_step"], 1)
                dve.wait_ge(s["place_step"], 2 * k + 2)
                dve.scalar_tensor_tensor(rec[:, :, FIELDS - 1], place_lo[:], float(T), place_hi[:], ALU.mult,
                                         ALU.add).then_inc(s["place_ready"], 1)
            dve.wait_ge(s["sorted_in"], 5 * 16)
            dve.tensor_copy(key_f[:], rec[:, :, KEY])
            dve.tensor_copy(after_f[:], after[:, :, KEY])
            dve.tensor_copy(eid_f[:], rec[:, :, EID])
            dve.tensor_copy(prior_f[:], prior[:, :, KEY]).then_inc(s["fields_step"], 1)
            dve.wait_ge(s["fields_step"], 1)
            dve.tensor_tensor(same_next[:], key_f[:], after_f[:], ALU.is_equal)
            dve.tensor_tensor(same_prior[:], key_f[0:1], prior_f[:], ALU.is_equal)
            dve.tensor_scalar(index[:, GATHER_SRC], key_f[:], float(N - 1), None, ALU.min)
            dve.tensor_scalar(index[:, GATHER_EDGE], eid_f[:], float(E - 1), None, ALU.min)
            dve.tensor_copy(index[:, GATHER_DST], rec[:, :, DST])
            dve.tensor_scalar(w1_f[:], rec[:, :, WEIGHT1].bitcast(F32), float(HD) ** -0.5, None, ALU.mult
                              ).then_inc(s["fields_step"], 1)
            dve.wait_ge(s["fields_step"], 2)
            dve.scalar_tensor_tensor(index[:, SCATTER], same_next[:], float(1 << 16), key_f[:], ALU.mult,
                                     ALU.add).then_inc(s["index_ready"], 1)

            def stats(m, edge):
                q, k = m.turn(2), m.back(DENSE)
                if edge:
                    dve.wait_ge(gathered[q], k.round(2, 16 * 2 * SUB, 1))
                else:
                    dve.wait_ge(x_in[m.turn(RX)], m.round(RX, 16, 1))
                sides = (x_sb[:, m.turn(RX)], xd[:, q])[:1 + edge]
                for side, t in enumerate(sides):
                    for j in range(SUB):
                        last = dve.bn_stats(bn[:, side, j], t[:, j])
                last.then_inc(s["stat_raw"], 1)
                dve.wait_ge(s["stat_raw"], m.lin(1, 1))
                dve.sem_inc(s["dve_passed"], 1)
                for side in range(len(sides)):
                    for j in range(SUB):
                        last = dve.bn_aggr(mv[:, q, side, j], bn[:, side, j])
                last.then_inc(s["stat"], 1)

            def normaliser(m, edge):
                q, sides = m.turn(2), 1 + edge
                dve.wait_ge(s["std_ready"], m.lin(1, 1))
                dve.reciprocal(rstd[:, q, 0:sides], std[:, q, 0:sides]).then_inc(s["rstd_step"], 1)
                dve.wait_ge(s["rstd_step"], m.lin(1, 1))
                dve.scalar_tensor_tensor(shift[:, q, 0:sides], mv[:, q, 0:sides, :, 0], -1.0, rstd[:, q, 0:sides],
                                         ALU.mult, ALU.mult).then_inc(s["rstd_ready"], 1)

            def messages(m):
                q, k = m.turn(2), m.back(DENSE)
                dve.tensor_copy(key_b[:], key_f[:, bass.ds(k.lin(SUB), SUB)].unsqueeze(2).to_broadcast([P, SUB, P])
                                ).then_inc(s["key_spread"], 1)
                dve.wait_ge(s["key_turned"], k.lin(1, 1))
                for j in range(SUB):
                    last = dve.tensor_scalar(equal[:, j], bank[7][:, j * P:(j + 1) * P],
                                             key_f[:, bass.ds(k.lin(SUB, j), 1)], None, ALU.is_equal)
                last.then_inc(s["equal_ready"], 1)
                dve.wait_ge(s["normed"], m.lin(1, 1))
                weight = rec[:, bass.ds(k.lin(SUB), SUB), WEIGHT0].bitcast(F32).unsqueeze(2).to_broadcast([P, SUB, D])
                dve.tensor_tensor(msg[:], msg[:], weight, ALU.mult).then_inc(s["weighted"], 1)
                dve.wait_ge(s["weighted"], k.lin(1, 1))
                for j in range(SUB):
                    row = msg[0:1, j]
                    if j or k.base:
                        dve.wait_ge(s["carried"], k.lin(SUB, j))
                        before_ = bank[7][0:1, 0:D] if j else carry_sb[:]
                        dve.scalar_tensor_tensor(row, before_, same_prior[:, bass.ds(k.lin(SUB, j), 1)], row,
                                                 ALU.mult, ALU.add).then_inc(s["msg_ready"], 1)
                    else:
                        dve.tensor_copy(row, row).then_inc(s["msg_ready"], 1)
                    dve.wait_ge(s["summed"], k.lin(SUB, j + 1))
                    if j == 0:
                        dve.wait_ge(s["turned"], m.lin(1, -1))
                    dve.scalar_tensor_tensor(h[:, q, j], h_self[:, j], self_w[:, 0:1], bank[6][:, 0:D], ALU.mult,
                                             ALU.add).then_inc(s["block_h"], 1)
                dve.tensor_copy(carry_sb[:], bank[7][0:1, 0:D]).then_inc(s["carry_saved"], 1)

            def add_b2(m):
                dve.wait_ge(s["l2_done"], m.lin(1, 1))
                for c in range(2):
                    last = dve.tensor_tensor(y[:, m.turn(2), 2 * c:2 * c + 2], bank[4 + c][:].rearrange("p (j f) -> p j f", j=2),
                                             b2_sb[:].unsqueeze(1).to_broadcast([P, 2, D]), ALU.add)
                last.then_inc(s["b2_added"], 1)

            def stats2(m):
                dve.wait_ge(s["relu_done"], m.lin(1, 1))
                for j in range(SUB):
                    last = dve.bn_stats(bn2[:, j], y[:, m.turn(2), j])
                last.then_inc(s["stat2_raw"], 1)
                dve.wait_ge(s["stat2_raw"], m.lin(1, 1))
                dve.sem_inc(s["dve_passed"], 1)
                for j in range(SUB):
                    last = dve.bn_aggr(mv2[:, m.turn(2), j], bn2[:, j])
                last.then_inc(s["stat2"], 1)

            def finish(m):
                q = m.turn(2)
                dve.wait_ge(s["std2_ready"], m.lin(1, 1))
                dve.reciprocal(rstd2[:, q], std2[:, q])
                for j in range(SUB):
                    last = dve.scalar_tensor_tensor(y[:, q, j], y[:, q, j], mv2[:, q, j, 0:1], scale_sb[:], ALU.subtract, ALU.mult)
                last.then_inc(s["scaled"], 1)
                if m.base >= DENSE + 2:
                    dve.wait_ge(scat_out[q], m.back(DENSE).round(2, 16 * SUB))
                elif m.base >= 2:
                    dve.wait_ge(stored[q], m.round(2, 32))
                dve.wait_ge(s["xo_made"], m.lin(1, 1))
                dve.wait_ge(s["scaled"], m.lin(1, 1))
                for j in range(SUB):
                    last = dve.scalar_tensor_tensor(fin[:, q, j], y[:, q, j], rstd2[:, q, j:j + 1], xo[:, m.turn(4), j],
                                                    ALU.mult, ALU.add)
                last.then_inc(s["finished"], 1)

            def turn(runs, edge):
                if runs(3):
                    add_b2(runs(3))
                if runs(-1):
                    stats(runs(-1), edge(-1))
                if runs(3):
                    stats2(runs(3))
                if runs(-1):
                    normaliser(runs(-1), edge(-1))
                if runs(3):
                    finish(runs(3))
                if runs(-1) and edge(-1):
                    messages(runs(-1))
            pipeline(dve, turn, **LAYER0)

            def stats1(k):
                q = k.turn(2)
                dve.wait_ge(b_gathered[q], k.round(2, 16 * 3 * SUB, 1))
                for side, t in enumerate((x_sb[:, k.turn(RX)], xd[:, q])):
                    for j in range(SUB):
                        last = dve.bn_stats(bn[:, side, j], t[:, j])
                last.then_inc(s["b_stat_raw"], 1)
                dve.wait_ge(s["b_stat_raw"], k.lin(1, 1))
                dve.sem_inc(s["dve_passed"], 1)
                for side in range(2):
                    for j in range(SUB):
                        last = dve.bn_aggr(mv[:, q, side, j], bn[:, side, j])
                last.then_inc(s["b_stat"], 1)

            def normaliser1(k):
                q = k.turn(2)
                dve.wait_ge(s["b_std_ready"], k.lin(1, 1))
                dve.reciprocal(rstd[:, q], std[:, q]).then_inc(s["b_rstd_step"], 1)
                dve.wait_ge(s["b_rstd_step"], k.lin(1, 1))
                dve.scalar_tensor_tensor(shift[:, q], mv[:, q, :, :, 0], -1.0, rstd[:, q],
                                         ALU.mult, ALU.mult).then_inc(s["b_rstd_ready"], 1)

            def equality1(k):
                dve.tensor_copy(key_b[:], key_f[:, bass.ds(k.lin(SUB), SUB)].unsqueeze(2).to_broadcast([P, SUB, P])
                                ).then_inc(s["b_key_spread"], 1)
                dve.wait_ge(s["b_key_turned"], k.lin(1, 1))
                for j in range(SUB):
                    last = dve.tensor_scalar(equal[:, j], bank[7][:, j * P:(j + 1) * P],
                                             key_f[:, bass.ds(k.lin(SUB, j), 1)], None, ALU.is_equal)
                last.then_inc(s["b_equal_ready"], 1)

            def attend(k, j):
                t = k.lin(SUB, j)
                t1 = k.lin(SUB, j + 1)
                qb, kvb = bank[2 + 2 * (j % 2)], bank[3 + 2 * (j % 2)]
                kv = kvb[:].rearrange("p (c w f) -> p c w f", c=CH, w=2)
                dve.wait_ge(s["b_qkv_done"], t1)
                dve.tensor_tensor(prod[:, j % 2], qb[:, 0:D], xo[:, k.turn(RX), j], ALU.mult).then_inc(s["b_qw"], 1)
                dve.wait_ge(s["b_qw"], t1)
                half = prod[:, j % 2].rearrange("p (c f) -> p c f", c=CH)
                dve.tensor_tensor(half, half, kv[:, :, 0], ALU.mult).then_inc(s["b_qwk"], 1)
                dve.wait_ge(s["b_qwk"], t1)
                dve.tensor_reduce(alpha[:, j % 2], prod[:, j % 2].rearrange("p (h f) -> p h f", h=H),
                                  mybir.AxisListType.X, ALU.add).then_inc(s["b_alpha"], 1)
                dve.wait_ge(s["b_alpha"], t1)
                dve.tensor_scalar(alpha_w[:, j % 2], alpha[:, j % 2], w1_f[:, bass.ds(t, 1)], None, ALU.mult).then_inc(s["b_alpha_w"], 1)
                dve.wait_ge(s["b_alpha_w"], t1)
                dve.tensor_tensor(msg[:, j].rearrange("p (c h f) -> p c h f", c=CH, h=2),
                                  alpha_w[:, j % 2].rearrange("p (c h) -> p c h", c=CH).unsqueeze(3).to_broadcast([P, CH, 2, HD]),
                                  kv[:, :, 1].rearrange("p c (h f) -> p c h f", h=2), ALU.mult).then_inc(s["b_msg"], 1)
                dve.wait_ge(s["b_msg"], t1)

            def total(k, j):
                q, row = k.turn(2), msg[0:1, j]
                if j or k.base:
                    dve.wait_ge(s["b_carried"], k.lin(SUB, j))
                    before_ = bank[7][0:1, 0:D] if j else carry_sb[:]
                    dve.scalar_tensor_tensor(row, before_, same_prior[:, bass.ds(k.lin(SUB, j), 1)], row,
                                             ALU.mult, ALU.add).then_inc(s["b_msg_ready"], 1)
                else:
                    dve.tensor_copy(row, row).then_inc(s["b_msg_ready"], 1)
                dve.wait_ge(s["b_summed"], k.lin(SUB, j + 1))
                if j == 0 and k.base >= 2:
                    dve.wait_ge(b_out[q], k.round(2, 16 * SUB))
                last = dve.tensor_tensor(fin[:, q, j], bank[6][:, 0:D], x_sb[:, k.turn(RX), j], ALU.add)
                last.then_inc(s["b_added"], 1)

            def turn1(runs, edge):
                if runs(-2):
                    stats1(runs(-2))
                k = runs(0)
                if k:
                    equality1(k)
                    attend(k, 0)
                    attend(k, 1)
                    total(k, 0)
                if runs(-2):
                    normaliser1(runs(-2))
                if k:
                    attend(k, 2)
                    total(k, 1)
                    attend(k, 3)
                    total(k, 2)
                    total(k, 3)
                    dve.tensor_copy(carry_sb[:], bank[7][0:1, 0:D]).then_inc(s["b_finished"], 1)
            pipeline(dve, turn1, **LAYER1)


        @block.scalar
        def _(act):
            def deviation(m, edge):
                q, sides = m.turn(2), 1 + edge
                act.wait_ge(s["stat"], m.lin(1, 1))
                act.activation(std[:, q, 0:sides], mv[:, q, 0:sides, :, 1], ACT.Sqrt, bias=ln_eps[:, 0:1]).then_inc(s["std_ready"], 1)

            def normalise(m, edge):
                q = m.turn(2)
                act.wait_ge(s["rstd_ready"], m.lin(1, 1))
                if edge:
                    if m.base > DENSE:
                        act.wait_ge(s["block_h"], m.back(DENSE).lin(SUB))
                        act.wait_ge(s["summed"], m.back(DENSE).lin(SUB))
                    pairs = ((x_sb[:, m.turn(RX)], h_self[:]), (xd[:, q], msg[:]))
                else:
                    if m.base >= 2:
                        act.wait_ge(s["turned"], m.lin(1, -1))
                    pairs = ((x_sb[:, m.turn(RX)], h[:, q]),)
                for side, (of, to) in enumerate(pairs):
                    for j in range(SUB):
                        last = act.activation(to[:, j], of[:, j], ACT.Relu, bias=shift[:, q, side, j:j + 1],
                                              scale=rstd[:, q, side, j:j + 1])
                last.then_inc(s["normed"], 1)

            def take_hT(m):
                act.wait_ge(s["turned"], m.lin(1, 1))
                if m.base >= 2:
                    act.wait_ge(s["l1_done"], m.lin(1, -1))
                for c in range(CH):
                    last = act.activation(hT[:, m.turn(2), c], bank[c][:], ACT.Copy)
                last.then_inc(s["hT_ready"], 1)

            def take_z1(m):
                act.wait_ge(s["l1_done"], m.lin(1, 1))
                if m.base >= 2:
                    act.wait_ge(s["l2_done"], m.lin(1, -1))
                for c in range(CH):
                    last = act.activation(z1[:, m.turn(2), c], bank[2 + c][:], ACT.Relu, bias=b1_sb[:, c:c + 1])
                last.then_inc(s["z1_ready"], 1)

            def relu(m):
                act.wait_ge(s["b2_added"], m.lin(1, 1))
                act.activation(y[:, m.turn(2)], y[:, m.turn(2)], ACT.Relu).then_inc(s["relu_done"], 1)

            def deviation2(m):
                act.wait_ge(s["stat2"], m.lin(1, 1))
                act.activation(std2[:, m.turn(2)], mv2[:, m.turn(2), :, 1], ACT.Sqrt, bias=post_eps[:, 0:1]).then_inc(s["std2_ready"], 1)

            def turn(runs, edge):
                if runs(0):
                    take_hT(runs(0))
                if runs(3):
                    relu(runs(3))
                if runs(-1):
                    deviation(runs(-1), edge(-1))
                if runs(1):
                    take_z1(runs(1))
                if runs(3):
                    deviation2(runs(3))
                if runs(-1):
                    normalise(runs(-1), edge(-1))
            act.wait_ge(s["w_ready"], 1)
            for c in range(CH):
                last = act.activation(w_qkv[:, c], bank[6 + c][:, 0:3 * P], ACT.Copy)
            last.then_inc(s["w_taken"], 1)
            act.wait_ge(s["const_in"], 7 * 16)
            act.wait_ge(s["index_ready"], 1)
            pipeline(act, turn, **LAYER0)

            def deviation1(k):
                q = k.turn(2)
                act.wait_ge(s["b_stat"], k.lin(1, 1))
                act.activation(std[:, q], mv[:, q, :, :, 1], ACT.Sqrt, bias=ln_eps[:, 0:1]).then_inc(s["b_std_ready"], 1)

            def normalise1(k):
                q = k.turn(2)
                act.wait_ge(s["b_rstd_ready"], k.lin(1, 1))
                if k.base >= 2:
                    act.wait_ge(s["b_turned"], k.lin(2, -2))
                for side, (of, to) in enumerate(((x_sb[:, k.turn(RX)], h[:, q]), (xd[:, q], y[:, q]))):
                    for j in range(SUB):
                        last = act.activation(to[:, j], of[:, j], ACT.Relu, bias=shift[:, q, side, j:j + 1],
                                              scale=rstd[:, q, side, j:j + 1])
                last.then_inc(s["b_normed"], 1)

            def take_turned1(k, side):
                act.wait_ge(s["b_turned"], k.lin(2, side + 1))
                if k.base >= 2:
                    act.wait_ge(s["b_qkv_done"], k.lin(SUB, -SUB))
                for c in range(CH):
                    last = act.activation((hT, z1)[side][:, k.turn(2), c], bank[c][:], ACT.Copy)
                last.then_inc(s["b_turned_taken"], 1)

            def turn1(runs, edge):
                if runs(-1):
                    take_turned1(runs(-1), 0)
                if runs(-2):
                    deviation1(runs(-2))
                if runs(-1):
                    take_turned1(runs(-1), 1)
                if runs(-2):
                    normalise1(runs(-2))
            pipeline(act, turn1, **LAYER1)


        @block.tensor
        def _(pe):
            pe.wait_ge(s["w_turned"], 16 * 3 * H)
            pe.wait_ge(s["const_made"], 3)
            for k in range(3):
                for c in range(CH):
                    mm = pe.transpose(bank[6 + c][:, k * P:(k + 1) * P], w_nat[:, k, c], ident[:])
            mm.then_inc(s["w_ready"], 1)
            for k in range(2):
                for t in range(1):
                    pe.wait_ge(s["onehot_ready"], k * T + 1)
                    pe.matmul(bank[2][:, 0:RADIX], all_ones[:], onehot[:, 2, :], start=True, stop=False)

                def count(t, k=k):
                    pe.wait_ge(s["onehot_ready"], t.lin(1, 1 + k * T))
                    pe.matmul(bank[2][:, 0:RADIX], all_ones[:], onehot[:, bass.ds(t.lin(1, 2), 1), :].squeeze(1),
                              start=False, stop=False)
                blocks(pe, 1, T - 1, count, unroll=2)
                pe.wait_ge(s["onehot_ready"], (k + 1) * T)
                pe.matmul(bank[2][:, 0:RADIX], all_ones[:], onehot[:, T + 1, :], start=False, stop=True).then_inc(s["counted"], 1)
                pe.wait_ge(s["bucket_ready"], k + 1)
                for half in range(2):
                    pe.matmul(bank[half][:, 0:RADIX], ident[:], bucket[:], start=True, stop=True)

                def rank_pair(g, k=k):
                    for half, (ready, read) in enumerate((("rank_a", "rank_a_read"), ("rank_b", "rank_b_read"))):
                        if g.base:
                            pe.wait_ge(s[read], g.lin(1, k * (T // 2)))
                        for add, lhs in enumerate((not_before, all_ones, before)):
                            mm = pe.matmul(bank[half][:, 0:RADIX], lhs[:],
                                           onehot[:, bass.ds(g.lin(2, half + add), 1), :].squeeze(1), start=False,
                                           stop=True, skip_group_check=True)
                        mm.then_inc(s[ready], 1)
                blocks(pe, 0, T // 2, rank_pair, unroll=2, peel=1)

            def turn_h(m):
                q = m.turn(2)
                if m.base >= DENSE:
                    pe.wait_ge(s["block_h"], m.back(DENSE).lin(SUB, SUB))
                else:
                    pe.wait_ge(s["normed"], m.lin(1, 1))
                if m.base:
                    pe.wait_ge(s["hT_ready"], m.n)
                for c in range(CH):
                    for j in range(SUB):
                        mm = pe.transpose(bank[c][:, j * P:(j + 1) * P], h[:, q, j, c * P:(c + 1) * P], ident[:])
                mm.then_inc(s["turned"], 1)

            def layer1(m):
                pe.wait_ge(s["hT_ready"], m.lin(1, 1))
                if m.base:
                    pe.wait_ge(s["z1_ready"], m.n)
                for o in range(CH):
                    for c in range(CH):
                        mm = pe.matmul(bank[2 + o][:], W1_sb[:, c, o * P:(o + 1) * P], hT[:, m.turn(2), c],
                                       start=(c == 0), stop=(c == CH - 1))
                mm.then_inc(s["l1_done"], 1)

            def layer2(m):
                pe.wait_ge(s["z1_ready"], m.lin(1, 1))
                if m.base:
                    pe.wait_ge(s["b2_added"], m.n)
                for j in range(SUB):
                    to = bank[4 + j // 2][:, j % 2 * D:(j % 2 + 1) * D]
                    for c in range(CH):
                        mm = pe.matmul(to, z1[:, m.turn(2), c, j * P:(j + 1) * P], W2_sb[:, c], start=(c == 0),
                                       stop=(c == CH - 1))
                mm.then_inc(s["l2_done"], 1)

            def sums(m):
                k = m.back(DENSE)
                if m.base == DENSE:
                    pe.wait_ge(s["w_taken"], 1)
                pe.wait_ge(s["key_spread"], k.lin(1, 1))
                if k.base:
                    pe.wait_ge(s["carry_saved"], k.n)
                for j in range(SUB):
                    mm = pe.transpose(bank[7][:, j * P:(j + 1) * P], key_b[:, j], ident[:])
                mm.then_inc(s["key_turned"], 1)
                pe.wait_ge(s["equal_ready"], k.lin(1, 1))
                for j in range(SUB):
                    pe.wait_ge(s["msg_ready"], k.lin(SUB, j + 1))
                    pe.matmul(bank[7][0:1, 0:D], equal[:, j, P - 1:P], msg[:, j], start=True, stop=True).then_inc(s["carried"], 1)
                    if j or k.base:
                        pe.wait_ge(s["block_h"], k.lin(SUB, j))
                    pe.matmul(bank[6][:, 0:D], equal[:, j], msg[:, j], start=True, stop=True).then_inc(s["summed"], 1)

            def turn(runs, edge):
                if runs(0):
                    turn_h(runs(0))
                if runs(1):
                    layer1(runs(1))
                if runs(2):
                    layer2(runs(2))
                if runs(-1) and edge(-1):
                    sums(runs(-1))
            pe.wait_ge(s["const_in"], 7 * 16)
            pipeline(pe, turn, **LAYER0)

            def turn1_rows(k, side):
                q = k.turn(2)
                pe.wait_ge(s["b_normed"], k.lin(1, 1))
                if side or k.base:
                    pe.wait_ge(s["b_turned_taken"], k.lin(2, side))
                for c in range(CH):
                    for j in range(SUB):
                        mm = pe.transpose(bank[c][:, j * P:(j + 1) * P], (h, y)[side][:, q, j, c * P:(c + 1) * P], ident[:])
                mm.then_inc(s["b_turned"], 1)

            def keys1(k):
                pe.wait_ge(s["b_key_spread"], k.lin(1, 1))
                for j in range(SUB):
                    mm = pe.transpose(bank[7][:, j * P:(j + 1) * P], key_b[:, j], ident[:])
                mm.then_inc(s["b_key_turned"], 1)

            def qkv(k, j):
                q = k.turn(2)
                if j == 0:
                    pe.wait_ge(s["b_turned_taken"], k.lin(2, 2))
                if j >= 2 or k.base:
                    pe.wait_ge(s["b_msg"], k.lin(SUB, j - 1))
                for c in range(CH):
                    pe.matmul(bank[2 + 2 * (j % 2)][:, c * P:(c + 1) * P], hT[:, q, c, j * P:(j + 1) * P], w_qkv[:, c, 0],
                              start=True, stop=True)
                    mm = pe.matmul(bank[3 + 2 * (j % 2)][:, c * D:(c + 1) * D], z1[:, q, c, j * P:(j + 1) * P],
                                   w_qkv[:, c, 1:3], start=True, stop=True)
                mm.then_inc(s["b_qkv_done"], 1)

            def sums1(k, j):
                if j == 0:
                    pe.wait_ge(s["b_equal_ready"], k.lin(1, 1))
                pe.wait_ge(s["b_msg_ready"], k.lin(SUB, j + 1))
                pe.matmul(bank[7][0:1, 0:D], equal[:, j, P - 1:P], msg[:, j], start=True, stop=True).then_inc(s["b_carried"], 1)
                if j or k.base:
                    pe.wait_ge(s["b_added"], k.lin(SUB, j))
                pe.matmul(bank[6][:, 0:D], equal[:, j], msg[:, j], start=True, stop=True).then_inc(s["b_summed"], 1)

            def turn1(runs, edge):
                k, ahead = runs(0), runs(-1)
                if ahead:
                    turn1_rows(ahead, 0)
                if k:
                    if k.base:
                        pe.wait_ge(s["b_finished"], k.n)
                    keys1(k)
                    qkv(k, 0)
                    qkv(k, 1)
                if ahead:
                    turn1_rows(ahead, 1)
                if k:
                    sums1(k, 0)
                    qkv(k, 2)
                    sums1(k, 1)
                    qkv(k, 3)
                    sums1(k, 2)
                    sums1(k, 3)
            pipeline(pe, turn1, **LAYER1)



def kernel(**inputs):
    import numpy as np
    import concourse.bacc as bacc
    from concourse.bass_utils import run_bass_kernel_spmd

    names = ["x", "src", "dst", "edge_attr_256", "edge_weight", "edge_weight1", "L0_gnn_W1", "L0_gnn_b1", "L0_gnn_W2",
             "L0_gnn_b2", "L0_gnn_eps", "L0_gnn_offset", "L0_gnn_scale", "L1_gnn_Wq", "L1_gnn_Wk", "L1_gnn_Wv"]
    nc = bacc.Bacc("TRN2", target_bir_lowering=False, num_devices=1)
    arrays, args = {}, []
    for name in names:
        a = np.ascontiguousarray(inputs[name])
        arrays[f"in_{name}"] = a
        args.append(nc.dram_tensor(f"in_{name}", a.shape, mybir.dt.from_np(a.dtype), kind="ExternalInput").ap())
    shape = inputs["x"].shape
    args.append(nc.dram_tensor("result", shape, F32, kind="ExternalOutput").ap())
    gnn_kernel(nc, *args)
    r = run_bass_kernel_spmd(nc, [arrays], core_ids=[0])
    return r.results[0]["result"]
```

```python
from contextlib import ExitStack

import concourse.bass as bass
from concourse import mybir

F32 = mybir.dt.float32
BF16 = mybir.dt.bfloat16
I32 = mybir.dt.int32
ALU = mybir.AluOpType
ACT = mybir.ActivationFunctionType

P = 128
SUB = 4
BLOCK = P * SUB
RADIX = 256
FIELDS = 8
KEY, DST, WEIGHT0, WEIGHT1, EID = range(5)
PAD_KEY = 65535
LN_EPS = 1e-5
POST_EPS = 1e-10


class At:

    def __init__(self, base, it=None, stride=0):
        self.base, self.it, self.stride = base, it, stride

    def back(self, n):
        return At(self.base - n, self.it, self.stride)

    def lin(self, scale, add=0):
        v = self.base * scale + add
        return v if self.it is None else self.it * (self.stride * scale) + v

    @property
    def n(self):
        return self.lin(1)

    def turn(self, ring):
        assert self.it is None or self.stride % ring == 0
        return self.base % ring

    def round(self, ring, scale=1, add=0):
        assert self.it is None or self.stride % ring == 0
        v = (self.base // ring + add) * scale
        return v if self.it is None else self.it * (self.stride // ring * scale) + v


def blocks(eng, first, end, body, unroll=4, peel=0):
    for i in range(first, first + peel):
        body(At(i))
    first += peel
    rounds = (end - first) // unroll
    if rounds >= 2:
        with eng.Fori(0, rounds) as it:
            for u in range(unroll):
                body(At(first + u, it, unroll))
        first += rounds * unroll
    for i in range(first, end):
        body(At(i))


def gnn_kernel(nc, x, src, dst, edge_attr, w0, w1, W1, b1, W2, b2, eps, offset, scale, Wq, Wk, Wv, out):
    N, D = x.shape
    E = src.shape[0]
    H, HD = Wq.shape[0], Wq.shape[1]
    CH = D // P
    T = -(-E // BLOCK) * SUB
    EP = T * P
    EPART = E // T
    assert EPART * T == E and N < PAD_KEY and D == 2 * P and H * HD == D
    DENSE = -(-N // BLOCK)
    EDGE = T // SUB
    ALL = DENSE + EDGE

    hidden = nc.dram_tensor("hidden", (N, D), F32, kind="Internal").ap()
    sorted_by = [nc.dram_tensor(f"sorted_{k}", (EP, FIELDS), I32, kind="Internal").ap() for k in range(2)]

    with ExitStack() as ctx:
        def sb(name, shape, dt=F32):
            return ctx.enter_context(nc.sbuf_tensor(name, shape, dt))

        def ps(name, shape):
            return ctx.enter_context(nc.psum_tensor(name, shape, F32))

        def sem(name):
            return ctx.enter_context(nc.semaphore(name))

        ident = sb("ident", [P, P])
        col_i, col_f = sb("col_i", [P, RADIX], I32), sb("col_f", [P, RADIX])
        row_i, row_f = sb("row_i", [P, 1], I32), sb("row_f", [P, 1])
        ones_f = sb("ones_f", [P, RADIX])
        all_ones, before, not_before = (sb(n, [P, P], BF16) for n in ("all_ones", "before", "not_before"))
        W1_sb, W2_sb = sb("W1_sb", [P, CH, D]), sb("W2_sb", [P, CH, D])
        b1_sb = sb("b1_sb", [P, CH])
        b2_rest, b2_bf, b2_parts = sb("b2_rest", [P, 2, D]), sb("b2_bf", [P, 3, D], BF16), sb("b2_parts", [P, D], BF16)
        b2_sb, offset_sb, scale_sb = sb("b2_sb", [P, D]), sb("offset_sb", [P, D]), sb("scale_sb", [P, D])
        eps_sb, self_w = sb("eps_sb", [P, 1]), sb("self_w", [P, 1])
        ln_eps, post_eps = sb("ln_eps", [P, 1]), sb("post_eps", [P, 1])
        w_nat = sb("w_nat", [P, 3, CH, P])
        w_qkv = sb("w_qkv", [P, CH, 3, P])

        raw = [sb(f"raw_{n}", [P, T], I32) for n in ("src", "dst", "w0", "w1", "eid")]
        rec = sb("rec", [P, T, FIELDS], I32)
        onehot = sb("onehot", [P, T + 2, RADIX], BF16)
        digit_i, digit_f = sb("digit_i", [P, T], I32), sb("digit_f", [P, T])
        counts, upto, bucket = sb("counts", [P, RADIX]), sb("upto", [P, RADIX]), sb("bucket", [P, RADIX])
        junk = sb("junk", [P, 2, RADIX])
        place_f = sb("place_f", [P, 2, SUB])
        place_i, place_lo, place_hi, place_row = (sb(n, [P, 2, SUB], I32) for n in ("place_i", "place_lo", "place_hi", "place_row"))
        moving = sb("moving", [P, 2, SUB, FIELDS], I32)
        after = sb("after", [P, T, FIELDS], I32)
        prior = sb("prior", [1, T, FIELDS], I32)
        key_f, after_f, same_next = sb("key_f", [P, T]), sb("after_f", [P, T]), sb("same_next", [P, T])
        prior_f, same_prior = sb("prior_f", [1, T]), sb("same_prior", [1, T])
        eid_f, w1_f = sb("eid_f", [P, T]), sb("w1_f", [P, T])
        GATHER_SRC, GATHER_DST, GATHER_EDGE, SCATTER = range(4)
        index = sb("index", [P, 4, T], I32)

        RX, RY = 4, 2
        x_sb = sb("x_sb", [P, RX, SUB, D])
        xo = sb("xo", [P, 4, SUB, D])
        xd = sb("xd", [P, RY, SUB, D])
        bn = sb("bn", [P, 2, SUB, 6])
        mv = sb("mv", [P, RY, 2, SUB, 2])
        std, rstd, shift = (sb(n, [P, RY, 2, SUB]) for n in ("std", "rstd", "shift"))
        h = sb("h", [P, RY, SUB, D])
        h_self = sb("h_self", [P, RY, SUB, D])
        msg = sb("msg", [P, RY, SUB, D])
        key_b = sb("key_b", [P, SUB, P])
        equal = sb("equal", [P, SUB, P])
        hT = sb("hT", [P, RY, CH, BLOCK])
        z1 = sb("z1", [P, RY, CH, BLOCK])
        y = sb("y", [P, RY, SUB, D])
        bn2 = sb("bn2", [P, SUB, 6])
        mv2 = sb("mv2", [P, RY, SUB, 2])
        std2, rstd2 = sb("std2", [P, RY, SUB]), sb("rstd2", [P, RY, SUB])
        fin = sb("fin", [P, RY, SUB, D])
        carry_sb = sb("carry_sb", [1, D])
        idx = sb("idx", [P, 2, 2, SUB], I32)
        idx1 = sb("idx1", [P, 2, 3, SUB], I32)
        prod = sb("prod", [P, 2, D])
        alpha, alpha_w = sb("alpha", [P, 2, H]), sb("alpha_w", [P, 2, H])
        idx_w = sb("idx_w", [P, 2, SUB], I32)

        bank = [ps(f"bank{k}", [P, 512]) for k in range(8)]

        s = {n: sem(n) for n in (
            "const_in", "edges_in", "iota_done", "const_made", "w_filled", "w_turned", "w_ready", "raw_ready",
            "rec_ready", "digit_ready", "onehot_ready", "counted", "bucket_step", "bucket_ready", "rank_summed",
            "rank_read", "place_step", "place_ready", "moved", "scattered_0", "scattered_1",
            "sorted_in", "fields_step", "index_ready",
            "stat_raw", "stat", "std_ready", "rstd_ready", "normed", "xo_made", "turned", "hT_ready",
            "l1_done", "z1_ready", "l2_done", "relu_done", "stat2_raw", "stat2", "std2_ready",
            "rstd2_ready", "scaled", "finished", "idx_ready", "key_spread", "key_turned", "equal_ready",
            "weighted", "edge_xo_made", "b2_step", "b2_ready", "carried", "summed", "carry_read", "block_h",
            "x_in0", "x_in1", "x_in2", "x_in3", "stored0", "stored1", "gathered0", "gathered1",
            "scat_idx_ready", "pool_passed", "w_taken", "b_normed", "b_idx_ready", "b_scat_ready", "b_stat_raw", "b_stat", "b_std_ready", "b_rstd_step", "b_rstd_ready", "b_key_spread", "b_key_turned", "b_equal_ready", "b_qkv_done", "b_qw", "b_qwk", "b_alpha", "b_alpha_w", "b_msg", "b_carry_saved", "b_carried", "b_msg_ready", "b_summed", "b_added", "b_turned", "b_turned_taken", "b_gathered0", "b_own0", "b_own1", "b_gathered1", "b_out0", "b_out1",
             "dve_passed", "scat_out0", "scat_out1", "rstd_step", "carry_saved", "msg_ready", "rows_in0", "rows_in1", "rstdB", "xdone",
        )}
        x_in = [s[f"x_in{k}"] for k in range(4)]
        stored = [s["stored0"], s["stored1"]]
        gathered = [s["gathered0"], s["gathered1"]]
        scattered = [s["scattered_0"], s["scattered_1"]]
        scat_out = [s["scat_out0"], s["scat_out1"]]
        b_gathered = [s["b_gathered0"], s["b_gathered1"]]
        b_own = [s["b_own0"], s["b_own1"]]
        b_out = [s["b_out0"], s["b_out1"]]

        block = ctx.enter_context(nc.Block())

        def block_rows(t, a):
            at = a if isinstance(a, int) else a.lin(BLOCK)
            return t[bass.ds(at, BLOCK), :].rearrange("(p j) f -> p j f", j=SUB)

        LAST = N - BLOCK
        DENSE_STORED = 2 * 16 * (DENSE // RY)
        assert DENSE % RY == 0

        HOT = 10
        SORT = {}
        turn_ = 0
        for k in range(2):
            for name, turns in (("digits", 1), ("hot", T // HOT), ("bucket", 1), ("rank", T // SUB)):
                SORT[name, k] = (turn_, turn_ + turns)
                turn_ += turns
            SORT["move", k] = (SORT["rank", k][0] + 1, turn_ + 1)
            SORT["reload", k] = (turn_ + 1, turn_ + 2)
            turn_ += 3
        SORT["fields", 1] = (turn_, turn_ + 1)
        assert T % HOT == 0 and turn_ < DENSE - 3

        def pipeline(eng, step, total, lags, edge_from=None, sort_steps=()):
            edge_from = total if edge_from is None else edge_from

            def sorting(i):
                return {name: k for (name, k), (a, b) in SORT.items() if name in sort_steps and a <= i < b}

            def flags(i):
                return {lag: (0 <= i - lag < total, i - lag >= edge_from) for lag in lags}, sorting(i)
            first, stop = lags[0], total + lags[-1]
            while first < stop:
                end = first + 1
                while end < stop and flags(end) == flags(first):
                    end += 1
                f, on = flags(first)

                def body(a, f=f, on=on):
                    args = (lambda lag: (a.back(lag) if f[lag][0] else None), lambda lag: f[lag][1])
                    if sort_steps:
                        args += (lambda name: ((on[name], a.back(SORT[name, on[name]][0])) if name in on else None),)
                    step(*args)
                peel = 4 if first < 8 else 2 if first == edge_from + lags[-1] or on else 0
                blocks(eng, first, end, body, peel=min(end - first, peel))
                first = end

        LAYER0 = dict(total=ALL, lags=range(-3, 4), edge_from=DENSE)
        LAYER1 = dict(total=EDGE, lags=range(-3, 2))

        @block.sync
        def _(sp):
            with nc.allow_non_contiguous_dma(reason="a column of biases"):
                sp.dma_start(b1_sb[:], b1.rearrange("(c p) -> p c", p=P)).then_inc(s["const_in"], 16)
            for to, of in ((W1_sb, W1), (W2_sb, W2)):
                sp.dma_start(to[:], of.rearrange("(c p) n -> p c n", p=P)).then_inc(s["const_in"], 16)
            for to, of in ((b2_sb, b2), (offset_sb, offset), (scale_sb, scale), (eps_sb, eps)):
                sp.dma_start(to[:], of.partition_broadcast(P)).then_inc(s["const_in"], 16)
            sp.wait_ge(s["raw_ready"], 1)
            for r, of in zip(raw, (src, dst, w0, w1)):
                of = of if len(of.shape) == 1 else of.rearrange("a b -> (a b)")
                of = of if of.dtype == I32 else of.bitcast(I32)
                sp.dma_start(r[0:EPART, :], of.rearrange("(p t) -> p t", t=T)).then_inc(s["edges_in"], 16)
            sp.wait_ge(s["w_filled"], 1)
            for k, W in enumerate((Wq, Wk, Wv)):
                for hh in range(H):
                    c, o = hh // 2, hh % 2 * HD
                    sp.dma_start(w_nat[o:o + HD, k, c, o:o + HD], W[hh]).then_inc(s["w_turned"], 16)
            def load(a, row=None):
                if a.base >= RX:
                    sp.wait_ge(s["normed"], a.lin(1, 1 - RX))
                    sp.wait_ge(s["xo_made"], a.lin(1, 1 - RX))
                sp.dma_start(x_sb[:, a.turn(RX)], block_rows(x, a if row is None else row)).then_inc(x_in[a.turn(RX)], 16)

            def store(a, row=None):
                sp.wait_ge(s["finished"], a.lin(1, 1))
                for t in (hidden, out):
                    sp.dma_start(block_rows(t, a if row is None else row), fin[:, a.turn(RY)]).then_inc(stored[a.turn(RY)], 16)

            LEAD = 7

            def load_and_store(a):
                store(a.back(LEAD))
                load(a)
            for i in range(LEAD):
                load(At(i))
            blocks(sp, LEAD, DENSE - 1, load_and_store)
            store(At(DENSE - 1 - LEAD))
            load(At(DENSE - 1), row=LAST)
            for i in range(DENSE - LEAD, DENSE - 1):
                store(At(i))
            sp.wait_ge(stored[(DENSE - 2) % RY], DENSE_STORED)
            store(At(DENSE - 1), row=LAST)

        @block.gpsimd
        def _(pool):
            pool.iota(col_i[:], [[1, RADIX]], base=0, channel_multiplier=0).then_inc(s["iota_done"], 1)
            pool.iota(row_i[:], [[0, 1]], base=0, channel_multiplier=1).then_inc(s["iota_done"], 1)
            pool.iota(raw[4][:], [[1, T]], base=0, channel_multiplier=T).then_inc(s["iota_done"], 1)

            def move(k, g):
                b = g.turn(2)
                if k or g.base >= 2:
                    pool.wait_ge(scattered[b], g.round(2, 16 * SUB, k * len(range(b, T // SUB, 2))))
                pool.tensor_copy(moving[:, b], rec[:, bass.ds(g.lin(SUB), SUB), :]).then_inc(s["moved"], 1)
                pool.wait_ge(s["moved"], g.lin(1, 1 + k * (T // SUB)))
                pool.wait_ge(s["place_ready"], g.lin(1, 1 + k * (T // SUB)))
                pool.sem_inc(s["pool_passed"], 1)
                for j in range(SUB):
                    pool.indirect_dma_start(sorted_by[k], bass.IndirectOffsetOnAxis(ap=place_row[:, b, j:j + 1], axis=0),
                                            moving[:, b, j, :], None).then_inc(scattered[b], 16)

            def reload(k, _):
                for b in range(2):
                    pool.wait_ge(scattered[b], 16 * SUB * (k + 1) * len(range(b, T // SUB, 2)))
                pool.dma_start(rec[:], sorted_by[k].rearrange("(p t) c -> p t c", t=T)).then_inc(s["sorted_in"], 16)
                if k == 1:
                    pool.wait_ge(s["raw_ready"], 2)
                    rows = sorted_by[1]
                    pool.dma_start(after[0:P - 1], rows[T:EP].rearrange("(p t) c -> p t c", t=T)).then_inc(s["sorted_in"], 16)
                    pool.dma_start(after[P - 1:P, 0:T - 1], rows[1:T].unsqueeze(0)).then_inc(s["sorted_in"], 16)
                    pool.dma_start(prior[0:1, 1:T], rows[EP - T:EP - 1].unsqueeze(0)).then_inc(s["sorted_in"], 16)

            def residual(m):
                pool.wait_ge(x_in[m.turn(RX)], m.round(RX, 16, 1))
                if m.base >= 4:
                    pool.wait_ge(s["finished"], m.lin(1, -3))
                pool.tensor_tensor(xo[:, m.turn(4)], x_sb[:, m.turn(RX)],
                                   offset_sb[:].unsqueeze(1).to_broadcast([P, SUB, D]), ALU.add).then_inc(s["xo_made"], 1)

            def gather(m):
                k, q = m.back(DENSE), m.turn(2)
                if m.base == DENSE:
                    pool.wait_ge(s["index_ready"], 1)
                pool.wait_ge(s["normed"], m.lin(1, -1))
                if m.base < DENSE + RX:
                    pool.wait_ge(s["xo_made"], m.lin(1, 1 - RX))
                else:
                    pool.wait_ge(s["edge_xo_made"], k.lin(1, 1 - RX))
                pool.tensor_copy(idx[:, q], index[:, 0:2, bass.ds(k.lin(SUB), SUB)]).then_inc(s["idx_ready"], 1)
                pool.wait_ge(s["idx_ready"], k.lin(1, 1))
                pool.sem_inc(s["pool_passed"], 1)
                for j in range(SUB):
                    for side, to in ((GATHER_SRC, x_sb[:, m.turn(RX), j]), (GATHER_DST, xd[:, q, j])):
                        pool.indirect_dma_start(to, None, x, bass.IndirectOffsetOnAxis(
                            ap=idx[:, q, side, j:j + 1], axis=0)).then_inc(gathered[q], 16)

            def scatter(m):
                k, q = m.back(DENSE), m.turn(2)
                if k.base >= 2:
                    pool.wait_ge(scat_out[q], k.round(2, 16 * SUB))
                pool.tensor_copy(idx_w[:, q], index[:, SCATTER, bass.ds(k.lin(SUB), SUB)]).then_inc(s["scat_idx_ready"], 1)
                pool.wait_ge(s["scat_idx_ready"], k.lin(1, 1))
                pool.wait_ge(s["finished"], m.lin(1, 1))
                pool.sem_inc(s["pool_passed"], 1)
                for j in range(SUB):
                    pool.indirect_dma_start(hidden, bass.IndirectOffsetOnAxis(ap=idx_w[:, q, j:j + 1], axis=0),
                                            fin[:, q, j], None, bounds_check=N - 1, oob_is_err=False).then_inc(scat_out[q], 16)

            pool.wait_ge(s["const_in"], 7 * 16)

            def turn(runs, edge, sort):
                if runs(-3) and edge(-3):
                    gather(runs(-3))
                if runs(0) and not edge(0):
                    residual(runs(0))
                if runs(3) and edge(3):
                    if runs(3).base == DENSE:
                        pool.wait_ge(stored[0], DENSE_STORED)
                        pool.wait_ge(stored[1], DENSE_STORED)
                    scatter(runs(3))
                for name, do in (("move", move), ("reload", reload)):
                    if sort(name):
                        do(*sort(name))
            pipeline(pool, turn, sort_steps=("move", "reload"), **LAYER0)

            def gather_ahead(k):
                q, r = k.turn(2), k.turn(RX)
                if k.base >= 2:
                    pool.wait_ge(s["b_normed"], k.lin(1, -1))
                if k.base >= RX:
                    pool.wait_ge(s["b_msg"], k.lin(SUB, SUB * (1 - RX)))
                pool.tensor_copy(idx1[:, q], index[:, 0:3, bass.ds(k.lin(SUB), SUB)]).then_inc(s["b_idx_ready"], 1)
                pool.wait_ge(s["b_idx_ready"], k.lin(1, 1))
                pool.sem_inc(s["pool_passed"], 1)
                for side, to, of in ((GATHER_DST, xd[:, q], hidden), (GATHER_EDGE, xo[:, r], edge_attr)):
                    for j in range(SUB):
                        pool.indirect_dma_start(to[:, j], None, of, bass.IndirectOffsetOnAxis(
                            ap=idx1[:, q, side, j:j + 1], axis=0)).then_inc(b_gathered[q], 16)

            def gather_own(k):
                q = k.turn(2)
                if k.base >= RX:
                    pool.wait_ge(s["b_added"], k.lin(SUB, SUB * (1 - RX)))
                    pool.sem_inc(s["pool_passed"], 1)
                for j in range(SUB):
                    pool.indirect_dma_start(x_sb[:, k.turn(RX), j], None, hidden, bass.IndirectOffsetOnAxis(
                        ap=idx1[:, q, GATHER_SRC, j:j + 1], axis=0)).then_inc(b_own[q], 16)

            def scatter1(k):
                q = k.turn(2)
                if k.base >= 2:
                    pool.wait_ge(b_out[q], k.round(2, 16 * SUB))
                pool.tensor_copy(idx_w[:, q], index[:, SCATTER, bass.ds(k.lin(SUB), SUB)]).then_inc(s["b_scat_ready"], 1)
                pool.wait_ge(s["b_scat_ready"], k.lin(1, 1))
                pool.wait_ge(s["b_added"], k.lin(SUB, SUB))
                pool.sem_inc(s["pool_passed"], 1)
                for j in range(SUB):
                    pool.indirect_dma_start(out, bass.IndirectOffsetOnAxis(ap=idx_w[:, q, j:j + 1], axis=0),
                                            fin[:, q, j], None, bounds_check=N - 1, oob_is_err=False).then_inc(b_out[q], 16)

            for q in range(2):
                pool.wait_ge(scat_out[(DENSE + q) % 2], 16 * SUB * len(range(q, EDGE, 2)))

            def turn1(runs, edge):
                if runs(-3):
                    gather_ahead(runs(-3))
                if runs(1):
                    scatter1(runs(1))
                if runs(-3):
                    gather_own(runs(-3))
            pipeline(pool, turn1, **LAYER1)
            for q in range(2):
                pool.wait_ge(b_out[q], 16 * SUB * len(range(q, EDGE, 2)))

        @block.vector
        def _(dve):
            for r, v in zip(raw[:4], (PAD_KEY, 0, 0, 0)):
                i = dve.memset(r[:], v)
            dve.memset(rec[:, :, 5:], 0)
            i.then_inc(s["raw_ready"], 1)
            dve.memset(w_nat[:], 0.0).then_inc(s["w_filled"], 1)
            dve.memset(after[:], -1)
            dve.memset(prior[:], -1).then_inc(s["raw_ready"], 1)
            dve.memset(ln_eps[:], LN_EPS)
            dve.memset(post_eps[:], POST_EPS)
            dve.memset(ones_f[:], 1.0)
            dve.memset(all_ones[:], 1.0)
            dve.memset(onehot[:, 0:2, :], 0.0)
            dve.wait_ge(s["iota_done"], 3)
            dve.tensor_copy(col_f[:], col_i[:]).then_inc(s["const_made"], 1)
            dve.tensor_copy(row_f[:], row_i[:]).then_inc(s["const_made"], 1)
            dve.wait_ge(s["const_made"], 2)
            dve.tensor_scalar(ident[:], col_f[:, 0:P], row_f[:, 0:1], None, ALU.is_equal)
            dve.tensor_scalar(before[:], col_f[:, 0:P], row_f[:, 0:1], None, ALU.is_gt)
            dve.tensor_scalar(not_before[:], col_f[:, 0:P], row_f[:, 0:1], None, ALU.is_le).then_inc(s["const_made"], 1)
            dve.wait_ge(s["edges_in"], 4 * 16)
            for c, r in enumerate(raw):
                i = dve.tensor_copy(rec[:, :, c], r[:])
            i.then_inc(s["rec_ready"], 1)
            dve.wait_ge(s["const_in"], 7 * 16)
            dve.tensor_scalar(self_w[:], eps_sb[:], 1.0, None, ALU.add)
            rest = b2_sb[:]
            dve.memset(b2_parts[:], 0.0)
            for part in range(3):
                dve.tensor_copy(b2_bf[:, part], rest).then_inc(s["b2_step"], 1)
                dve.wait_ge(s["b2_step"], 2 * part + 1)
                if part < 2:
                    dve.tensor_tensor(b2_rest[:, part], rest, b2_bf[:, part], ALU.subtract).then_inc(s["b2_step"], 1)
                    dve.wait_ge(s["b2_step"], 2 * part + 2)
                    rest = b2_rest[:, part]
            for part in range(3):
                one = slice(32 * part, 32 * part + 1)
                last = dve.tensor_copy(b2_parts[one, :], b2_bf[one, part])
            last.then_inc(s["b2_ready"], 1)

            def digits(k, _):
                if k:
                    dve.wait_ge(s["sorted_in"], 16)
                else:
                    dve.wait_ge(s["rec_ready"], 1)
                dve.tensor_scalar(digit_i[:], rec[:, :, KEY], 8 * k, RADIX - 1, ALU.logical_shift_right,
                                  ALU.bitwise_and).then_inc(s["digit_ready"], 1)
                dve.wait_ge(s["digit_ready"], 2 * k + 1)
                dve.tensor_copy(digit_f[:], digit_i[:]).then_inc(s["digit_ready"], 1)
                dve.wait_ge(s["digit_ready"], 2 * k + 2)

            def one_hots(k, g):
                for u in range(HOT):
                    last = dve.tensor_scalar(onehot[:, bass.ds(g.lin(HOT, u + 2), 1), :].squeeze(1), col_f[:],
                                             digit_f[:, bass.ds(g.lin(HOT, u), 1)], None, ALU.is_equal)
                last.then_inc(s["onehot_ready"], 1)

            def bucket_starts(k, _):
                dve.wait_ge(s["counted"], (k + 1) * (T // HOT))
                dve.tensor_copy(counts[:], bank[6][:, 0:RADIX]).then_inc(s["bucket_step"], 1)
                dve.wait_ge(s["bucket_step"], 2 * k + 1)
                dve.tensor_tensor_scan(upto[:], ones_f[:], counts[:], 0.0, ALU.mult, ALU.add).then_inc(s["bucket_step"], 1)
                dve.wait_ge(s["bucket_step"], 2 * k + 2)
                dve.tensor_tensor(bucket[:], upto[:], counts[:], ALU.subtract).then_inc(s["bucket_ready"], 1)

            def read_ranks(k, g, pair):
                dve.wait_ge(s["rank_summed"], g.lin(2, 1 + pair + k * (T // 2)))
                for half in range(2):
                    u = 2 * pair + half
                    last = dve.scalar_tensor_tensor(
                        junk[:, half], bank[6 + half][:, 0:RADIX], 1.0, onehot[:, bass.ds(g.lin(SUB, 2 + u), 1), :].squeeze(1),
                        ALU.mult, ALU.mult, accum_out=place_f[:, g.turn(2), u:u + 1])
                last.then_inc(s["rank_read"], 1)

            def rows_of_places(k, g):
                b, before_ = g.turn(2), k * (T // SUB)
                dve.wait_ge(s["rank_read"], g.lin(2, 2 + k * (T // 2)))
                dve.tensor_copy(place_i[:, b], place_f[:, b]).then_inc(s["place_step"], 1)
                dve.wait_ge(s["place_step"], g.lin(2, 1 + 2 * before_))
                dve.tensor_scalar(place_lo[:, b], place_i[:, b], P - 1, None, ALU.bitwise_and)
                dve.tensor_scalar(place_hi[:, b], place_i[:, b], P.bit_length() - 1, None, ALU.logical_shift_right
                                  ).then_inc(s["place_step"], 1)
                if k or g.base >= 2:
                    dve.wait_ge(scattered[b], g.round(2, 16 * SUB, k * len(range(b, T // SUB, 2))))
                dve.wait_ge(s["place_step"], g.lin(2, 2 + 2 * before_))
                dve.scalar_tensor_tensor(place_row[:, b], place_lo[:, b], float(T), place_hi[:, b], ALU.mult,
                                         ALU.add).then_inc(s["place_ready"], 1)

            def fields(k, _):
                dve.wait_ge(s["sorted_in"], 5 * 16)
                dve.tensor_copy(key_f[:], rec[:, :, KEY])
                dve.tensor_copy(after_f[:], after[:, :, KEY])
                dve.tensor_copy(eid_f[:], rec[:, :, EID])
                dve.tensor_copy(prior_f[:], prior[:, :, KEY]).then_inc(s["fields_step"], 1)
                dve.wait_ge(s["fields_step"], 1)
                dve.tensor_tensor(same_next[:], key_f[:], after_f[:], ALU.is_equal)
                dve.tensor_tensor(same_prior[:], key_f[0:1], prior_f[:], ALU.is_equal)
                dve.tensor_scalar(index[:, GATHER_SRC], key_f[:], float(N - 1), None, ALU.min)
                dve.tensor_scalar(index[:, GATHER_EDGE], eid_f[:], float(E - 1), None, ALU.min)
                dve.tensor_copy(index[:, GATHER_DST], rec[:, :, DST])
                dve.tensor_scalar(w1_f[:], rec[:, :, WEIGHT1].bitcast(F32), float(HD) ** -0.5, None, ALU.mult
                                  ).then_inc(s["fields_step"], 1)
                dve.wait_ge(s["fields_step"], 2)
                dve.scalar_tensor_tensor(index[:, SCATTER], same_next[:], float(1 << 16), key_f[:], ALU.mult,
                                         ALU.add).then_inc(s["index_ready"], 1)

            def row_stats(m, edge, side):
                q, k = m.turn(2), m.back(DENSE)
                if side == 0:
                    if edge:
                        dve.wait_ge(gathered[q], k.round(2, 16 * 2 * SUB, 1))
                    else:
                        dve.wait_ge(x_in[m.turn(RX)], m.round(RX, 16, 1))
                of = xd[:, q] if side else x_sb[:, m.turn(RX)]
                for j in range(SUB):
                    last = dve.bn_stats(bn[:, side, j], of[:, j])
                if side == edge:
                    last.then_inc(s["stat_raw"], 1)

            def join_stats(m, edge):
                dve.wait_ge(s["stat_raw"], m.lin(1, 1))
                dve.sem_inc(s["dve_passed"], 1)
                for side in range(1 + edge):
                    for j in range(SUB):
                        last = dve.bn_aggr(mv[:, m.turn(2), side, j], bn[:, side, j])
                last.then_inc(s["stat"], 1)

            def inverse(m, edge):
                q, sides = m.turn(2), 1 + edge
                dve.wait_ge(s["std_ready"], m.lin(1, 1))
                dve.reciprocal(rstd[:, q, 0:sides], std[:, q, 0:sides]).then_inc(s["rstd_step"], 1)

            def shifts(m, edge):
                q, sides = m.turn(2), 1 + edge
                dve.wait_ge(s["rstd_step"], m.lin(1, 1))
                dve.scalar_tensor_tensor(shift[:, q, 0:sides], mv[:, q, 0:sides, :, 0], -1.0, rstd[:, q, 0:sides],
                                         ALU.mult, ALU.mult).then_inc(s["rstd_ready"], 1)

            def spread_keys(m):
                k = m.back(DENSE)
                dve.tensor_copy(key_b[:], key_f[:, bass.ds(k.lin(SUB), SUB)].unsqueeze(2).to_broadcast([P, SUB, P])
                                ).then_inc(s["key_spread"], 1)

            def edge_residual(m):
                dve.wait_ge(s["finished"], m.lin(1, -3))
                dve.tensor_tensor(xo[:, m.turn(4)], x_sb[:, m.turn(RX)],
                                  offset_sb[:].unsqueeze(1).to_broadcast([P, SUB, D]), ALU.add).then_inc(s["edge_xo_made"], 1)

            def weigh(m):
                k, q = m.back(DENSE), m.turn(2)
                dve.wait_ge(s["normed"], m.lin(1, 1))
                weight = rec[:, bass.ds(k.lin(SUB), SUB), WEIGHT0].bitcast(F32).unsqueeze(2).to_broadcast([P, SUB, D])
                dve.tensor_tensor(msg[:, q], msg[:, q], weight, ALU.mult).then_inc(s["weighted"], 1)

            def equality(m):
                k = m.back(DENSE)
                dve.wait_ge(s["key_turned"], k.lin(1, 1))
                for j in range(SUB):
                    last = dve.tensor_scalar(equal[:, j], bank[7][:, j * P:(j + 1) * P],
                                             key_f[:, bass.ds(k.lin(SUB, j), 1)], None, ALU.is_equal)
                last.then_inc(s["equal_ready"], 1)

            def join_carry(m, j):
                k, row = m.back(DENSE), msg[0:1, m.turn(2), j]
                dve.wait_ge(s["weighted"], k.lin(1, 1))
                if j or k.base:
                    if j:
                        dve.wait_ge(s["summed"], k.lin(SUB, j))
                    else:
                        dve.wait_ge(s["carry_saved"], k.n)
                    before_ = bank[6 + (j - 1) % 2][0:1, D:2 * D] if j else carry_sb[:]
                    dve.scalar_tensor_tensor(row, before_, same_prior[:, bass.ds(k.lin(SUB, j), 1)], row,
                                             ALU.mult, ALU.add).then_inc(s["msg_ready"], 1)
                else:
                    dve.tensor_copy(row, row).then_inc(s["msg_ready"], 1)

            def own_and_sum(m, j):
                k, q = m.back(DENSE), m.turn(2)
                dve.wait_ge(s["summed"], k.lin(SUB, j + 1))
                if j == 0:
                    dve.wait_ge(s["turned"], m.lin(1, -1))
                dve.scalar_tensor_tensor(h[:, q, j], h_self[:, q, j], self_w[:, 0:1], bank[6 + j % 2][:, 0:D],
                                         ALU.mult, ALU.add).then_inc(s["block_h"], 1)

            def save_carry(m):
                dve.wait_ge(s["summed"], m.back(DENSE).lin(SUB, SUB))
                dve.tensor_copy(carry_sb[:], bank[7][0:1, D:2 * D]).then_inc(s["carry_saved"], 1)

            def out_stats(m):
                dve.wait_ge(s["relu_done"], m.lin(1, 1))
                for j in range(SUB):
                    last = dve.bn_stats(bn2[:, j], y[:, m.turn(2), j])
                last.then_inc(s["stat2_raw"], 1)

            def join_out_stats(m):
                dve.wait_ge(s["stat2_raw"], m.lin(1, 1))
                dve.sem_inc(s["dve_passed"], 1)
                for j in range(SUB):
                    last = dve.bn_aggr(mv2[:, m.turn(2), j], bn2[:, j])
                last.then_inc(s["stat2"], 1)

            def scale_out(m):
                q = m.turn(2)
                dve.wait_ge(s["stat2"], m.lin(1, 1))
                for j in range(SUB):
                    last = dve.scalar_tensor_tensor(y[:, q, j], y[:, q, j], mv2[:, q, j, 0:1], scale_sb[:], ALU.subtract, ALU.mult)
                last.then_inc(s["scaled"], 1)

            def out_inverse(m):
                dve.wait_ge(s["std2_ready"], m.lin(1, 1))
                dve.reciprocal(rstd2[:, m.turn(2)], std2[:, m.turn(2)]).then_inc(s["rstd2_ready"], 1)

            def finish(m):
                q = m.turn(2)
                if m.base >= DENSE + 2:
                    dve.wait_ge(scat_out[q], m.back(DENSE).round(2, 16 * SUB))
                elif m.base >= 2:
                    dve.wait_ge(stored[q], m.round(2, 32))
                if m.base >= DENSE:
                    dve.wait_ge(s["edge_xo_made"], m.back(DENSE).lin(1, 1))
                else:
                    dve.wait_ge(s["xo_made"], m.lin(1, 1))
                dve.wait_ge(s["scaled"], m.lin(1, 1))
                dve.wait_ge(s["rstd2_ready"], m.lin(1, 1))
                for j in range(SUB):
                    last = dve.scalar_tensor_tensor(fin[:, q, j], y[:, q, j], rstd2[:, q, j:j + 1], xo[:, m.turn(4), j],
                                                    ALU.mult, ALU.add)
                last.then_inc(s["finished"], 1)

            def turn(runs, edge, sort):
                m, f, g = runs(-2), runs(3), runs(-1) if edge(-1) else None
                if runs(0) and edge(0):
                    edge_residual(runs(0))
                if g:
                    weigh(g)
                if m:
                    row_stats(m, edge(-2), 0)
                if g:
                    equality(g)
                    join_carry(g, 0)
                if f:
                    out_stats(f)
                if g:
                    join_carry(g, 1)
                    own_and_sum(g, 0)
                if m:
                    if edge(-2):
                        row_stats(m, True, 1)
                    join_stats(m, edge(-2))
                if g:
                    join_carry(g, 2)
                    own_and_sum(g, 1)
                if f:
                    join_out_stats(f)
                if sort("rank"):
                    read_ranks(*sort("rank"), pair=0)
                if m:
                    inverse(m, edge(-2))
                    if edge(-2):
                        spread_keys(m)
                    shifts(m, edge(-2))
                if f:
                    scale_out(f)
                if g:
                    join_carry(g, 3)
                    own_and_sum(g, 2)
                if f:
                    out_inverse(f)
                if g:
                    save_carry(g)
                    own_and_sum(g, 3)
                if f:
                    finish(f)
                if sort("rank"):
                    read_ranks(*sort("rank"), pair=1)
                    rows_of_places(*sort("rank"))
                for name, do in (("digits", digits), ("hot", one_hots), ("bucket", bucket_starts), ("fields", fields)):
                    if sort(name):
                        do(*sort(name))
            pipeline(dve, turn, sort_steps=("digits", "hot", "bucket", "rank", "fields"), **LAYER0)

            def stats1(k, side):
                q = k.turn(2)
                if side:
                    dve.wait_ge(b_gathered[q], k.round(2, 16 * 2 * SUB, 1))
                else:
                    dve.wait_ge(b_own[q], k.round(2, 16 * SUB, 1))
                of = xd[:, q] if side else x_sb[:, k.turn(RX)]
                for j in range(SUB):
                    last = dve.bn_stats(bn[:, side, j], of[:, j])
                last.then_inc(s["b_stat_raw"], 1)

            def join_stats1(k):
                dve.wait_ge(s["b_stat_raw"], k.lin(2, 2))
                dve.sem_inc(s["dve_passed"], 1)
                for side in range(2):
                    for j in range(SUB):
                        last = dve.bn_aggr(mv[:, k.turn(2), side, j], bn[:, side, j])
                last.then_inc(s["b_stat"], 1)

            def inverse1(k):
                q = k.turn(2)
                dve.wait_ge(s["b_std_ready"], k.lin(1, 1))
                dve.reciprocal(rstd[:, q], std[:, q]).then_inc(s["b_rstd_step"], 1)

            def shifts1(k):
                q = k.turn(2)
                dve.wait_ge(s["b_rstd_step"], k.lin(1, 1))
                dve.scalar_tensor_tensor(shift[:, q], mv[:, q, :, :, 0], -1.0, rstd[:, q],
                                         ALU.mult, ALU.mult).then_inc(s["b_rstd_ready"], 1)

            def spread_keys1(k):
                dve.tensor_copy(key_b[:], key_f[:, bass.ds(k.lin(SUB), SUB)].unsqueeze(2).to_broadcast([P, SUB, P])
                                ).then_inc(s["b_key_spread"], 1)

            def equality1(k):
                dve.wait_ge(s["b_key_turned"], k.lin(1, 1))
                for j in range(SUB):
                    last = dve.tensor_scalar(equal[:, j], bank[7][:, j * P:(j + 1) * P],
                                             key_f[:, bass.ds(k.lin(SUB, j), 1)], None, ALU.is_equal)
                last.then_inc(s["b_equal_ready"], 1)

            def kv_banks(j):
                return bank[3 + 2 * (j % 2)][:].rearrange("p (c w f) -> p c w f", c=CH, w=2)

            def attend(k, pair):
                tiles = (2 * pair, 2 * pair + 1)
                for j in tiles:
                    dve.wait_ge(s["b_qkv_done"], k.lin(SUB, j + 1))
                    dve.tensor_tensor(prod[:, j % 2], bank[2 + 2 * (j % 2)][:, 0:D], xo[:, k.turn(RX), j], ALU.mult
                                      ).then_inc(s["b_qw"], 1)
                for j in tiles:
                    dve.wait_ge(s["b_qw"], k.lin(SUB, j + 1))
                    half = prod[:, j % 2].rearrange("p (c f) -> p c f", c=CH)
                    dve.tensor_tensor(half, half, kv_banks(j)[:, :, 0], ALU.mult).then_inc(s["b_qwk"], 1)
                for j in tiles:
                    dve.wait_ge(s["b_qwk"], k.lin(SUB, j + 1))
                    dve.tensor_reduce(alpha[:, j % 2], prod[:, j % 2].rearrange("p (h f) -> p h f", h=H),
                                      mybir.AxisListType.X, ALU.add).then_inc(s["b_alpha"], 1)
                for j in tiles:
                    dve.wait_ge(s["b_alpha"], k.lin(SUB, j + 1))
                    dve.tensor_scalar(alpha_w[:, j % 2], alpha[:, j % 2], w1_f[:, bass.ds(k.lin(SUB, j), 1)], None,
                                      ALU.mult).then_inc(s["b_alpha_w"], 1)

            def message(k, pair):
                for j in (2 * pair, 2 * pair + 1):
                    dve.wait_ge(s["b_alpha_w"], k.lin(SUB, j + 1))
                    dve.tensor_tensor(msg[:, k.turn(2), j].rearrange("p (c h f) -> p c h f", c=CH, h=2),
                                      alpha_w[:, j % 2].rearrange("p (c h) -> p c h", c=CH).unsqueeze(3).to_broadcast([P, CH, 2, HD]),
                                      kv_banks(j)[:, :, 1].rearrange("p c (h f) -> p c h f", h=2), ALU.mult).then_inc(s["b_msg"], 1)

            def join_carry1(k, j):
                q = k.turn(2)
                row = msg[0:1, q, j]
                dve.wait_ge(s["b_msg"], k.lin(SUB, j + 1))
                if j or k.base:
                    if j:
                        dve.wait_ge(s["b_summed"], k.lin(SUB, j))
                    else:
                        dve.wait_ge(s["b_carry_saved"], k.n)
                    before_ = bank[6 + (j - 1) % 2][0:1, D:2 * D] if j else carry_sb[:]
                    dve.scalar_tensor_tensor(row, before_, same_prior[:, bass.ds(k.lin(SUB, j), 1)], row,
                                             ALU.mult, ALU.add).then_inc(s["b_msg_ready"], 1)
                else:
                    dve.tensor_copy(row, row).then_inc(s["b_msg_ready"], 1)

            def total(k, j):
                q = k.turn(2)
                dve.wait_ge(s["b_summed"], k.lin(SUB, j + 1))
                if j == 0 and k.base >= 2:
                    dve.wait_ge(b_out[q], k.round(2, 16 * SUB))
                last = dve.tensor_tensor(fin[:, q, j], bank[6 + j % 2][:, 0:D], x_sb[:, k.turn(RX), j], ALU.add)
                last.then_inc(s["b_added"], 1)

            def save_carry1(k):
                dve.wait_ge(s["b_summed"], k.lin(SUB, SUB))
                dve.tensor_copy(carry_sb[:], bank[7][0:1, D:2 * D]).then_inc(s["b_carry_saved"], 1)

            def turn1(runs, edge):
                m, k, g = runs(-2), runs(0), runs(1)
                if g:
                    equality1(g)
                    join_carry1(g, 0)
                if k:
                    attend(k, 0)
                if g:
                    join_carry1(g, 1)
                    total(g, 0)
                if k:
                    message(k, 0)
                if m:
                    stats1(m, 1)
                if g:
                    join_carry1(g, 2)
                    total(g, 1)
                if m:
                    stats1(m, 0)
                if k:
                    attend(k, 1)
                if g:
                    join_carry1(g, 3)
                    total(g, 2)
                if m:
                    join_stats1(m)
                if k:
                    message(k, 1)
                    spread_keys1(k)
                if m:
                    inverse1(m)
                if g:
                    save_carry1(g)
                if m:
                    shifts1(m)
                if g:
                    total(g, 3)
            pipeline(dve, turn1, **LAYER1)


        @block.scalar
        def _(act):
            def deviation(m, edge):
                q, sides = m.turn(2), 1 + edge
                act.wait_ge(s["stat"], m.lin(1, 1))
                act.activation(std[:, q, 0:sides], mv[:, q, 0:sides, :, 1], ACT.Sqrt, bias=ln_eps[:, 0:1]).then_inc(s["std_ready"], 1)

            def normalise(m, edge):
                q = m.turn(2)
                act.wait_ge(s["rstd_ready"], m.lin(1, 1))
                if edge:
                    if m.base >= DENSE + 2:
                        act.wait_ge(s["block_h"], m.back(DENSE).lin(SUB, -SUB))
                        act.wait_ge(s["summed"], m.back(DENSE).lin(SUB, -SUB))
                    pairs = ((x_sb[:, m.turn(RX)], h_self[:, q]), (xd[:, q], msg[:, q]))
                else:
                    if m.base >= 2:
                        act.wait_ge(s["turned"], m.lin(1, -1))
                    pairs = ((x_sb[:, m.turn(RX)], h[:, q]),)
                for side, (of, to) in enumerate(pairs):
                    for j in range(SUB):
                        last = act.activation(to[:, j], of[:, j], ACT.Relu, bias=shift[:, q, side, j:j + 1],
                                              scale=rstd[:, q, side, j:j + 1])
                last.then_inc(s["normed"], 1)

            def take_hT(m):
                act.wait_ge(s["turned"], m.lin(1, 1))
                if m.base >= 2:
                    act.wait_ge(s["l1_done"], m.lin(1, -1))
                for c in range(CH):
                    last = act.activation(hT[:, m.turn(2), c], bank[c][:], ACT.Copy)
                last.then_inc(s["hT_ready"], 1)

            def take_z1(m):
                act.wait_ge(s["l1_done"], m.lin(1, 1))
                if m.base >= 2:
                    act.wait_ge(s["l2_done"], m.lin(1, -1))
                for c in range(CH):
                    last = act.activation(z1[:, m.turn(2), c], bank[2 + c][:], ACT.Relu, bias=b1_sb[:, c:c + 1])
                last.then_inc(s["z1_ready"], 1)

            def relu(m):
                act.wait_ge(s["l2_done"], m.lin(1, 1))
                if m.base >= 2:
                    act.wait_ge(s["finished"], m.lin(1, -1))
                for c in range(2):
                    last = act.activation(y[:, m.turn(2), 2 * c:2 * c + 2], bank[4 + c][:].rearrange("p (j f) -> p j f", j=2),
                                          ACT.Relu)
                last.then_inc(s["relu_done"], 1)

            def deviation2(m):
                act.wait_ge(s["stat2"], m.lin(1, 1))
                act.activation(std2[:, m.turn(2)], mv2[:, m.turn(2), :, 1], ACT.Sqrt, bias=post_eps[:, 0:1]).then_inc(s["std2_ready"], 1)

            def turn(runs, edge, sort=None):
                if runs(3):
                    relu(runs(3))
                if runs(0):
                    take_hT(runs(0))
                if runs(-2):
                    deviation(runs(-2), edge(-2))
                if runs(3):
                    deviation2(runs(3))
                if runs(1):
                    take_z1(runs(1))
                if runs(-2):
                    normalise(runs(-2), edge(-2))
            act.wait_ge(s["w_ready"], 1)
            for c in range(CH):
                last = act.activation(w_qkv[:, c], bank[6 + c][:, 0:3 * P], ACT.Copy)
            last.then_inc(s["w_taken"], 1)
            act.wait_ge(s["const_in"], 7 * 16)
            pipeline(act, turn, **LAYER0)

            def deviation1(k):
                q = k.turn(2)
                act.wait_ge(s["b_stat"], k.lin(1, 1))
                act.activation(std[:, q], mv[:, q, :, :, 1], ACT.Sqrt, bias=ln_eps[:, 0:1]).then_inc(s["b_std_ready"], 1)

            def normalise1(k):
                q = k.turn(2)
                act.wait_ge(s["b_rstd_ready"], k.lin(1, 1))
                if k.base >= 2:
                    act.wait_ge(s["b_turned"], k.lin(2, -2))
                for side, (of, to) in enumerate(((x_sb[:, k.turn(RX)], h[:, q]), (xd[:, q], y[:, q]))):
                    for j in range(SUB):
                        last = act.activation(to[:, j], of[:, j], ACT.Relu, bias=shift[:, q, side, j:j + 1],
                                              scale=rstd[:, q, side, j:j + 1])
                last.then_inc(s["b_normed"], 1)

            def take_turned1(k, side):
                act.wait_ge(s["b_turned"], k.lin(2, side + 1))
                if k.base >= 2:
                    act.wait_ge(s["b_qkv_done"], k.lin(SUB, -SUB))
                for c in range(CH):
                    last = act.activation((hT, z1)[side][:, k.turn(2), c], bank[c][:], ACT.Copy)
                last.then_inc(s["b_turned_taken"], 1)

            def turn1(runs, edge):
                if runs(-1):
                    take_turned1(runs(-1), 0)
                if runs(-2):
                    deviation1(runs(-2))
                if runs(-1):
                    take_turned1(runs(-1), 1)
                if runs(-2):
                    normalise1(runs(-2))
            pipeline(act, turn1, **LAYER1)


        @block.tensor
        def _(pe):
            pe.wait_ge(s["w_turned"], 16 * 3 * H)
            pe.wait_ge(s["const_made"], 3)
            for k in range(3):
                for c in range(CH):
                    mm = pe.transpose(bank[6 + c][:, k * P:(k + 1) * P], w_nat[:, k, c], ident[:])
            mm.then_inc(s["w_ready"], 1)
            def count(k, g):
                pe.wait_ge(s["onehot_ready"], g.lin(1, 1 + k * (T // HOT)))
                first = g.it is None and g.base == 0
                if first and k == 0:
                    pe.wait_ge(s["w_taken"], 1)
                for u in range(HOT):
                    mm = pe.matmul(bank[6][:, 0:RADIX], all_ones[:], onehot[:, bass.ds(g.lin(HOT, 2 + u), 1), :].squeeze(1),
                                   start=first and u == 0, stop=True, skip_group_check=True)
                mm.then_inc(s["counted"], 1)

            def start_ranks(k, _):
                pe.wait_ge(s["bucket_ready"], k + 1)
                for half in range(2):
                    pe.matmul(bank[6 + half][:, 0:RADIX], ident[:], bucket[:], start=True, stop=True)

            def rank_pair(k, g, pair):
                if k or g.base or pair:
                    pe.wait_ge(s["rank_read"], g.lin(2, pair + k * (T // 2)))
                for half in range(2):
                    for add, lhs in enumerate((not_before, all_ones, before)):
                        mm = pe.matmul(bank[6 + half][:, 0:RADIX], lhs[:],
                                       onehot[:, bass.ds(g.lin(SUB, 2 * pair + half + add), 1), :].squeeze(1), start=False,
                                       stop=True, skip_group_check=True)
                mm.then_inc(s["rank_summed"], 1)

            def turn_h(m):
                q = m.turn(2)
                if m.base >= DENSE:
                    pe.wait_ge(s["block_h"], m.back(DENSE).lin(SUB, SUB))
                else:
                    pe.wait_ge(s["normed"], m.lin(1, 1))
                if m.base:
                    pe.wait_ge(s["hT_ready"], m.n)
                for c in range(CH):
                    for j in range(SUB):
                        mm = pe.transpose(bank[c][:, j * P:(j + 1) * P], h[:, q, j, c * P:(c + 1) * P], ident[:])
                mm.then_inc(s["turned"], 1)

            def layer1(m, o):
                if o == 0:
                    pe.wait_ge(s["hT_ready"], m.lin(1, 1))
                    if m.base:
                        pe.wait_ge(s["z1_ready"], m.n)
                for c in range(CH):
                    mm = pe.matmul(bank[2 + o][:], W1_sb[:, c, o * P:(o + 1) * P], hT[:, m.turn(2), c],
                                   start=(c == 0), stop=(c == CH - 1))
                if o == CH - 1:
                    mm.then_inc(s["l1_done"], 1)

            def layer2(m, half):
                if half == 0:
                    pe.wait_ge(s["z1_ready"], m.lin(1, 1))
                    if m.base:
                        pe.wait_ge(s["relu_done"], m.n)
                for j in (2 * half, 2 * half + 1):
                    to = bank[4 + half][:, j % 2 * D:(j % 2 + 1) * D]
                    pe.matmul(to, all_ones[:], b2_parts[:], start=True, stop=False)
                    for c in range(CH):
                        mm = pe.matmul(to, z1[:, m.turn(2), c, j * P:(j + 1) * P], W2_sb[:, c], start=False,
                                       stop=(c == CH - 1))
                if half:
                    mm.then_inc(s["l2_done"], 1)

            def turn_keys(m):
                k = m.back(DENSE)
                pe.wait_ge(s["key_spread"], k.lin(1, 1))
                if k.base:
                    pe.wait_ge(s["carry_saved"], k.n)
                    pe.wait_ge(s["block_h"], k.lin(SUB))
                for j in range(SUB):
                    mm = pe.transpose(bank[7][:, j * P:(j + 1) * P], key_b[:, j], ident[:])
                mm.then_inc(s["key_turned"], 1)

            def sums(m, j):
                k, q = m.back(DENSE), m.turn(2)
                if j == 0:
                    pe.wait_ge(s["equal_ready"], k.lin(1, 1))
                pe.wait_ge(s["msg_ready"], k.lin(SUB, j + 1))
                if j >= 2 or k.base:
                    pe.wait_ge(s["block_h"], k.lin(SUB, j - 1))
                pe.matmul(bank[6 + j % 2][0:1, D:2 * D], equal[:, j, P - 1:P], msg[:, q, j], start=True, stop=True)
                pe.matmul(bank[6 + j % 2][:, 0:D], equal[:, j], msg[:, q, j], start=True, stop=True).then_inc(s["summed"], 1)

            def turn(runs, edge, sort):
                g = runs(-1) if edge(-1) else None
                if sort("rank") and sort("rank")[1].base == 0 and sort("rank")[1].it is None:
                    start_ranks(*sort("rank"))
                if g:
                    turn_keys(g)
                if runs(0):
                    turn_h(runs(0))
                if sort("rank"):
                    rank_pair(*sort("rank"), pair=0)
                if g:
                    sums(g, 0)
                if runs(1):
                    layer1(runs(1), 0)
                if g:
                    sums(g, 1)
                if runs(1):
                    layer1(runs(1), 1)
                if sort("rank"):
                    rank_pair(*sort("rank"), pair=1)
                if g:
                    sums(g, 2)
                if runs(2):
                    layer2(runs(2), 0)
                if g:
                    sums(g, 3)
                if runs(2):
                    layer2(runs(2), 1)
                if sort("hot"):
                    count(*sort("hot"))
            pe.wait_ge(s["b2_ready"], 1)
            pipeline(pe, turn, sort_steps=("hot", "rank"), **LAYER0)

            def turn1_rows(k, side):
                q = k.turn(2)
                pe.wait_ge(s["b_normed"], k.lin(1, 1))
                if side or k.base:
                    pe.wait_ge(s["b_turned_taken"], k.lin(2, side))
                for c in range(CH):
                    for j in range(SUB):
                        mm = pe.transpose(bank[c][:, j * P:(j + 1) * P], (h, y)[side][:, q, j, c * P:(c + 1) * P], ident[:])
                mm.then_inc(s["b_turned"], 1)

            def turn_keys1(k):
                pe.wait_ge(s["b_key_spread"], k.lin(1, 1))
                if k.base:
                    pe.wait_ge(s["b_carry_saved"], k.n)
                    pe.wait_ge(s["b_added"], k.lin(SUB))
                for j in range(SUB):
                    mm = pe.transpose(bank[7][:, j * P:(j + 1) * P], key_b[:, j], ident[:])
                mm.then_inc(s["b_key_turned"], 1)

            def qkv(k, j):
                q = k.turn(2)
                if j == 0:
                    pe.wait_ge(s["b_turned_taken"], k.lin(2, 2))
                if j >= 2 or k.base:
                    pe.wait_ge(s["b_msg"], k.lin(SUB, j - 1))
                for c in range(CH):
                    pe.matmul(bank[2 + 2 * (j % 2)][:, c * P:(c + 1) * P], hT[:, q, c, j * P:(j + 1) * P], w_qkv[:, c, 0],
                              start=True, stop=True)
                    mm = pe.matmul(bank[3 + 2 * (j % 2)][:, c * D:(c + 1) * D], z1[:, q, c, j * P:(j + 1) * P],
                                   w_qkv[:, c, 1:3], start=True, stop=True)
                mm.then_inc(s["b_qkv_done"], 1)

            def sums1(k, j):
                q = k.turn(2)
                if j == 0:
                    pe.wait_ge(s["b_equal_ready"], k.lin(1, 1))
                pe.wait_ge(s["b_msg_ready"], k.lin(SUB, j + 1))
                if j >= 2 or k.base:
                    pe.wait_ge(s["b_added"], k.lin(SUB, j - 1))
                pe.matmul(bank[6 + j % 2][0:1, D:2 * D], equal[:, j, P - 1:P], msg[:, q, j], start=True, stop=True)
                pe.matmul(bank[6 + j % 2][:, 0:D], equal[:, j], msg[:, q, j], start=True, stop=True).then_inc(s["b_summed"], 1)

            def turn1(runs, edge):
                ahead, k, g = runs(-1), runs(0), runs(1)
                if g:
                    turn_keys1(g)
                if k:
                    qkv(k, 0)
                    qkv(k, 1)
                if g:
                    sums1(g, 0)
                if ahead:
                    turn1_rows(ahead, 0)
                if g:
                    sums1(g, 1)
                if ahead:
                    turn1_rows(ahead, 1)
                if k:
                    qkv(k, 2)
                if g:
                    sums1(g, 2)
                if k:
                    qkv(k, 3)
                if g:
                    sums1(g, 3)
            pipeline(pe, turn1, **LAYER1)



def kernel(**inputs):
    import numpy as np
    import concourse.bacc as bacc
    from concourse.bass_utils import run_bass_kernel_spmd

    names = ["x", "src", "dst", "edge_attr_256", "edge_weight", "edge_weight1", "L0_gnn_W1", "L0_gnn_b1", "L0_gnn_W2",
             "L0_gnn_b2", "L0_gnn_eps", "L0_gnn_offset", "L0_gnn_scale", "L1_gnn_Wq", "L1_gnn_Wk", "L1_gnn_Wv"]
    nc = bacc.Bacc("TRN2", target_bir_lowering=False, num_devices=1)
    arrays, args = {}, []
    for name in names:
        a = np.ascontiguousarray(inputs[name])
        arrays[f"in_{name}"] = a
        args.append(nc.dram_tensor(f"in_{name}", a.shape, mybir.dt.from_np(a.dtype), kind="ExternalInput").ap())
    shape = inputs["x"].shape
    args.append(nc.dram_tensor("result", shape, F32, kind="ExternalOutput").ap())
    gnn_kernel(nc, *args)
    r = run_bass_kernel_spmd(nc, [arrays], core_ids=[0])
    return r.results[0]["result"]
```

```python
from contextlib import ExitStack

import concourse.bass as bass
from concourse import mybir

F32 = mybir.dt.float32
BF16 = mybir.dt.bfloat16
I32 = mybir.dt.int32
ALU = mybir.AluOpType
ACT = mybir.ActivationFunctionType

P = 128
SUB = 4
BLOCK = P * SUB
RADIX = 256
FIELDS = 8
KEY, DST, WEIGHT0, WEIGHT1, EID = range(5)
PAD_KEY = 65535
LN_EPS = 1e-5
POST_EPS = 1e-10


class At:

    def __init__(self, base, it=None, stride=0):
        self.base, self.it, self.stride = base, it, stride

    def back(self, n):
        return At(self.base - n, self.it, self.stride)

    def lin(self, scale, add=0):
        v = self.base * scale + add
        return v if self.it is None else self.it * (self.stride * scale) + v

    @property
    def n(self):
        return self.lin(1)

    def turn(self, ring):
        assert self.it is None or self.stride % ring == 0
        return self.base % ring

    def round(self, ring, scale=1, add=0):
        assert self.it is None or self.stride % ring == 0
        v = (self.base // ring + add) * scale
        return v if self.it is None else self.it * (self.stride // ring * scale) + v


def blocks(eng, first, end, body, unroll=4, peel=0):
    for i in range(first, first + peel):
        body(At(i))
    first += peel
    rounds = (end - first) // unroll
    if rounds >= 2:
        with eng.Fori(0, rounds) as it:
            for u in range(unroll):
                body(At(first + u, it, unroll))
        first += rounds * unroll
    for i in range(first, end):
        body(At(i))


def gnn_kernel(nc, x, src, dst, edge_attr, w0, w1, W1, b1, W2, b2, eps, offset, scale, Wq, Wk, Wv, out):
    N, D = x.shape
    E = src.shape[0]
    H, HD = Wq.shape[0], Wq.shape[1]
    CH = D // P
    T = -(-E // BLOCK) * SUB
    EP = T * P
    EPART = E // T
    assert EPART * T == E and N < PAD_KEY and D == 2 * P and H * HD == D
    DENSE = -(-N // BLOCK)
    EDGE = T // SUB
    ALL = DENSE + EDGE

    hidden = nc.dram_tensor("hidden", (N, D), F32, kind="Internal").ap()
    attr_sorted = nc.dram_tensor("attr_sorted", (EP, D), F32, kind="Internal").ap()
    sorted_by = [nc.dram_tensor(f"sorted_{k}", (EP, FIELDS), I32, kind="Internal").ap() for k in range(2)]

    with ExitStack() as ctx:
        def sb(name, shape, dt=F32):
            return ctx.enter_context(nc.sbuf_tensor(name, shape, dt))

        def ps(name, shape):
            return ctx.enter_context(nc.psum_tensor(name, shape, F32))

        def sem(name):
            return ctx.enter_context(nc.semaphore(name))

        ident = sb("ident", [P, P])
        col_i, col_f = sb("col_i", [P, RADIX], I32), sb("col_f", [P, RADIX])
        row_i, row_f = sb("row_i", [P, 1], I32), sb("row_f", [P, 1])
        ones_f = sb("ones_f", [P, RADIX])
        all_ones, before, not_before = (sb(n, [P, P], BF16) for n in ("all_ones", "before", "not_before"))
        W1_sb, W2_sb = sb("W1_sb", [P, CH, D]), sb("W2_sb", [P, CH, D])
        b1_sb = sb("b1_sb", [P, CH])
        b2_rest, b2_bf, b2_parts = sb("b2_rest", [P, 2, D]), sb("b2_bf", [P, 3, D], BF16), sb("b2_parts", [P, D], BF16)
        b2_sb, offset_sb, scale_sb = sb("b2_sb", [P, D]), sb("offset_sb", [P, D]), sb("scale_sb", [P, D])
        eps_sb, self_w = sb("eps_sb", [P, 1]), sb("self_w", [P, 1])
        ln_eps, post_eps = sb("ln_eps", [P, 1]), sb("post_eps", [P, 1])
        w_nat = sb("w_nat", [P, 3, CH, P])
        w_qkv = sb("w_qkv", [P, CH, 3, P])

        raw = [sb(f"raw_{n}", [P, T], I32) for n in ("src", "dst", "w0", "w1", "eid")]
        rec = sb("rec", [P, T, FIELDS], I32)
        onehot = sb("onehot", [P, T + 2, RADIX], BF16)
        digit_i, digit_f = sb("digit_i", [P, T], I32), sb("digit_f", [P, T])
        counts, upto, bucket = sb("counts", [P, RADIX]), sb("upto", [P, RADIX]), sb("bucket", [P, RADIX])
        junk = sb("junk", [P, 2, RADIX])
        place_f = sb("place_f", [P, 2, SUB])
        place_i, place_lo, place_hi, place_row = (sb(n, [P, 2, SUB], I32) for n in ("place_i", "place_lo", "place_hi", "place_row"))
        moving = sb("moving", [P, 2, SUB, FIELDS], I32)
        after = sb("after", [P, T, FIELDS], I32)
        prior = sb("prior", [1, T, FIELDS], I32)
        key_f, after_f, same_next = sb("key_f", [P, T]), sb("after_f", [P, T]), sb("same_next", [P, T])
        prior_f, same_prior = sb("prior_f", [1, T]), sb("same_prior", [1, T])
        eid_f, w1_f = sb("eid_f", [P, T]), sb("w1_f", [P, T])
        GATHER_SRC, GATHER_DST, GATHER_EDGE, SCATTER = range(4)
        index = sb("index", [P, 4, T], I32)

        RX, RY = 4, 2
        x_sb = sb("x_sb", [P, RX, SUB, D])
        xo = sb("xo", [P, 4, SUB, D])
        xd = sb("xd", [P, RY, SUB, D])
        bn = sb("bn", [P, 2, SUB, 6])
        mv = sb("mv", [P, RY, 2, SUB, 2])
        std, rstd, shift = (sb(n, [P, RY, 2, SUB]) for n in ("std", "rstd", "shift"))
        h = sb("h", [P, RY, SUB, D])
        h_self = sb("h_self", [P, RY, SUB, D])
        msg = sb("msg", [P, RY, SUB, D])
        key_b = sb("key_b", [P, SUB, P])
        equal = sb("equal", [P, SUB, P])
        hT = sb("hT", [P, RY, CH, BLOCK])
        z1 = sb("z1", [P, RY, CH, BLOCK])
        y = sb("y", [P, RY, SUB, D])
        bn2 = sb("bn2", [P, SUB, 6])
        mv2 = sb("mv2", [P, RY, SUB, 2])
        std2, rstd2 = sb("std2", [P, RY, SUB]), sb("rstd2", [P, RY, SUB])
        fin = sb("fin", [P, RY, SUB, D])
        carry_sb = sb("carry_sb", [1, D])
        idx = sb("idx", [P, 2, 2, SUB], I32)
        idx1 = sb("idx1", [P, 2, 2, SUB], I32)
        idx_attr = sb("idx_attr", [P, 2, SUB], I32)
        attr_sb = sb("attr_sb", [P, 2, SUB, D])
        prod = sb("prod", [P, 2, D])
        alpha, alpha_w = sb("alpha", [P, 2, H]), sb("alpha_w", [P, 2, H])
        idx_w = sb("idx_w", [P, 2, SUB], I32)

        bank = [ps(f"bank{k}", [P, 512]) for k in range(8)]

        s = {n: sem(n) for n in (
            "const_in", "edges_in", "iota_done", "const_made", "w_filled", "self_w_ready", "w_in", "w_ready", "raw_ready",
            "rec_ready", "digit_ready", "onehot_ready", "onehot_ready_pool", "counted", "bucket_step",
            "bucket_ready", "rank_summed", "rank_read", "place_step", "place_ready", "moved", "sorted_in",
            "fields_step", "index_ready",
            "stat_raw", "stat", "std_ready", "rstd_ready", "normed", "xo_made", "turned", "hT_ready", "l1_done",
            "z1_ready", "l2_done", "relu_done", "stat2_raw", "stat2", "std2_ready", "rstd2_ready", "scaled",
            "finished", "idx_ready", "key_spread", "key_turned", "equal_ready", "weighted", "other_normed",
            "edge_xo_made", "b2_step", "b2_ready", "summed", "block_h", "scat_idx_ready", "pool_passed", "w_taken",
            "attr_idx_ready", "dve_passed", "rstd_step", "carry_saved", "msg_ready",
            "att_normed", "att_idx_ready", "att_scat_ready", "att_stat_raw", "att_stat", "att_std_ready", "att_rstd_step",
            "att_rstd_ready", "att_key_spread", "att_key_turned", "att_equal_ready", "att_qkv_done", "att_qw", "att_qwk",
            "att_alpha", "att_alpha_w", "att_msg", "att_carry_saved", "att_msg_ready", "att_summed", "att_added", "att_turned",
            "att_turned_taken",
        )}

        def ring_sems(name, ring):
            return [sem(f"{name}{r}") for r in range(ring)]
        scattered = ring_sems("scattered", 2)
        x_in, stored = ring_sems("x_in", RX), ring_sems("stored", RY)
        gathered, scat_out = ring_sems("gathered", 2), ring_sems("scat_out", 2)
        attr_got, attr_stored = ring_sems("attr_got", 2), ring_sems("attr_stored", 2)
        attr_in = ring_sems("attr_in", RX)
        att_gathered, att_own, att_out = ring_sems("att_gathered", 2), ring_sems("att_own", 2), ring_sems("att_out", 2)

        def kv_bank(j):
            return bank[3 + 2 * (j % 2)][:].rearrange("p (c w f) -> p c w f", c=CH, w=2)

        block = ctx.enter_context(nc.Block())

        def block_rows(t, a):
            at = a if isinstance(a, int) else a.lin(BLOCK)
            return t[bass.ds(at, BLOCK), :].rearrange("(p j) f -> p j f", j=SUB)

        LAST = N - BLOCK
        DENSE_STORED = 2 * 16 * (DENSE // RY)
        assert DENSE % RY == 0

        HOT = 20
        HOT_POOL = 6
        SORT = {}
        turn_ = -3
        for k in range(2):
            for name, turns in (("digits", 1), ("hot", T // HOT), ("bucket", 1), ("rank", T // SUB)):
                SORT[name, k] = (turn_, turn_ + turns)
                turn_ += turns
            SORT["move", k] = (SORT["rank", k][0] + 1, turn_ + 1)
            SORT["reload", k] = (turn_ + 1, turn_ + 2)
            turn_ += 3
        SORT["fields", 1] = (turn_, turn_ + 1)
        SORT["attrs", 1] = (turn_ + 1, turn_ + 1 + EDGE)
        SORT["attrs_out", 1] = (turn_ + 2, turn_ + 2 + EDGE)
        assert T % HOT == 0 and turn_ < DENSE - 3 and turn_ + EDGE < DENSE

        def pipeline(eng, step, total, lags, edge_from=None, sort_steps=()):
            edge_from = total if edge_from is None else edge_from

            def sorting(i):
                return {name: k for (name, k), (a, b) in SORT.items() if name in sort_steps and a <= i < b}

            def flags(i):
                return {lag: (0 <= i - lag < total, i - lag >= edge_from) for lag in lags}, sorting(i)
            first, stop = lags[0], total + lags[-1]
            while first < stop:
                end = first + 1
                while end < stop and flags(end) == flags(first):
                    end += 1
                f, on = flags(first)

                def body(a, f=f, on=on):
                    args = (lambda lag: (a.back(lag) if f[lag][0] else None), lambda lag: f[lag][1])
                    if sort_steps:
                        args += (lambda name: ((on[name], a.back(SORT[name, on[name]][0])) if name in on else None),)
                    step(*args)
                peel = 4 if first < 8 else 2 if first == edge_from + lags[-1] or on else 0
                blocks(eng, first, end, body, peel=min(end - first, peel))
                first = end

        LAYER0 = dict(total=ALL, lags=range(-3, 4), edge_from=DENSE)
        LAYER1 = dict(total=EDGE, lags=range(-3, 2))

        @block.sync
        def _(sp):
            def load(a, row=None):
                if a.base >= RX:
                    sp.wait_ge(s["normed"], a.lin(1, 1 - RX))
                    sp.wait_ge(s["xo_made"], a.lin(1, 1 - RX))
                sp.dma_start(x_sb[:, a.turn(RX)], block_rows(x, a if row is None else row)).then_inc(x_in[a.turn(RX)], 16)

            def store(a, row=None):
                sp.wait_ge(s["finished"], a.lin(1, 1))
                for t in (hidden, out):
                    sp.dma_start(block_rows(t, a if row is None else row), fin[:, a.turn(RY)]).then_inc(stored[a.turn(RY)], 16)

            LEAD = 7

            def load_and_store(a):
                store(a.back(LEAD))
                load(a)
            sp.wait_ge(s["raw_ready"], 1)
            for r, of in zip(raw, (src, dst, w0, w1)):
                of = of if len(of.shape) == 1 else of.rearrange("a b -> (a b)")
                of = of if of.dtype == I32 else of.bitcast(I32)
                sp.dma_start(r[0:EPART, :], of.rearrange("(p t) -> p t", t=T)).then_inc(s["edges_in"], 16)
            load(At(0))
            load(At(1))
            with nc.allow_non_contiguous_dma(reason="a column of biases"):
                sp.dma_start(b1_sb[:], b1.rearrange("(c p) -> p c", p=P)).then_inc(s["const_in"], 16)
            for to, of in ((W1_sb, W1), (W2_sb, W2)):
                sp.dma_start(to[:], of.rearrange("(c p) n -> p c n", p=P)).then_inc(s["const_in"], 16)
            for to, of in ((b2_sb, b2), (offset_sb, offset), (scale_sb, scale), (eps_sb, eps)):
                sp.dma_start(to[:], of.partition_broadcast(P)).then_inc(s["const_in"], 16)
            for i in range(2, LEAD):
                load(At(i))
            sp.wait_ge(s["w_filled"], 1)
            for k, W in enumerate((Wq, Wk, Wv)):
                for hh in range(H):
                    c, o = hh // 2, hh % 2 * HD
                    sp.dma_start(w_nat[o:o + HD, k, c, o:o + HD], W[hh]).then_inc(s["w_in"], 16)
            blocks(sp, LEAD, DENSE - 1, load_and_store)
            store(At(DENSE - 1 - LEAD))
            load(At(DENSE - 1), row=LAST)
            for i in range(DENSE - LEAD, DENSE - 1):
                store(At(i))
            sp.wait_ge(stored[(DENSE - 2) % RY], DENSE_STORED)
            store(At(DENSE - 1), row=LAST)

            for b in range(2):
                sp.wait_ge(attr_stored[b], 16 * len(range(b, EDGE, 2)))
            sp.wait_ge(s["finished"], ALL)

            def load_attrs(k):
                if k.base >= RX:
                    sp.wait_ge(s["att_msg"], k.lin(SUB, SUB * (1 - RX)))
                sp.dma_start(xo[:, k.turn(RX)], block_rows(attr_sorted, k)).then_inc(attr_in[k.turn(RX)], 16)
            blocks(sp, 0, EDGE, load_attrs, peel=RX)

        @block.gpsimd
        def _(pool):
            pool.iota(col_i[:], [[1, RADIX]], base=0, channel_multiplier=0).then_inc(s["iota_done"], 1)
            pool.iota(row_i[:], [[0, 1]], base=0, channel_multiplier=1).then_inc(s["iota_done"], 1)
            pool.iota(raw[4][:], [[1, T]], base=0, channel_multiplier=T).then_inc(s["iota_done"], 1)

            def one_hots(k, g):
                if k == 0 and g.base == 0:
                    pool.wait_ge(s["const_made"], 3)
                pool.wait_ge(s["digit_ready"], 2 * k + 2)
                for u in range(HOT - HOT_POOL, HOT):
                    last = pool.tensor_scalar(onehot[:, bass.ds(g.lin(HOT, u + 2), 1), :].squeeze(1), col_f[:],
                                              digit_f[:, bass.ds(g.lin(HOT, u), 1)], None, ALU.is_equal)
                last.then_inc(s["onehot_ready_pool"], 1)

            def move(k, g):
                b = g.turn(2)
                if k or g.base >= 2:
                    pool.wait_ge(scattered[b], g.round(2, 16 * SUB, k * len(range(b, T // SUB, 2))))
                pool.tensor_copy(moving[:, b], rec[:, bass.ds(g.lin(SUB), SUB), :]).then_inc(s["moved"], 1)
                pool.wait_ge(s["moved"], g.lin(1, 1 + k * (T // SUB)))
                pool.wait_ge(s["place_ready"], g.lin(1, 1 + k * (T // SUB)))
                pool.sem_inc(s["pool_passed"], 1)
                for j in range(SUB):
                    pool.indirect_dma_start(sorted_by[k], bass.IndirectOffsetOnAxis(ap=place_row[:, b, j:j + 1], axis=0),
                                            moving[:, b, j, :], None).then_inc(scattered[b], 16)

            def reload(k, _):
                for b in range(2):
                    pool.wait_ge(scattered[b], 16 * SUB * (k + 1) * len(range(b, T // SUB, 2)))
                pool.dma_start(rec[:], sorted_by[k].rearrange("(p t) c -> p t c", t=T)).then_inc(s["sorted_in"], 16)
                if k == 1:
                    pool.wait_ge(s["raw_ready"], 2)
                    rows = sorted_by[1]
                    pool.dma_start(after[0:P - 1], rows[T:EP].rearrange("(p t) c -> p t c", t=T)).then_inc(s["sorted_in"], 16)
                    pool.dma_start(after[P - 1:P, 0:T - 1], rows[1:T].unsqueeze(0)).then_inc(s["sorted_in"], 16)
                    pool.dma_start(prior[0:1, 1:T], rows[EP - T:EP - 1].unsqueeze(0)).then_inc(s["sorted_in"], 16)

            def sort_attrs(_, g):
                b = g.turn(2)
                if g.base == 0:
                    pool.wait_ge(s["index_ready"], 1)
                if g.base >= 2:
                    pool.wait_ge(attr_stored[b], g.round(2, 16))
                pool.tensor_copy(idx_attr[:, b], index[:, GATHER_EDGE, bass.ds(g.lin(SUB), SUB)]).then_inc(s["attr_idx_ready"], 1)
                pool.wait_ge(s["attr_idx_ready"], g.lin(1, 1))
                pool.sem_inc(s["pool_passed"], 1)
                for j in range(SUB):
                    pool.indirect_dma_start(attr_sb[:, b, j], None, edge_attr, bass.IndirectOffsetOnAxis(
                        ap=idx_attr[:, b, j:j + 1], axis=0)).then_inc(attr_got[b], 16)

            def residual(m):
                if m.base == 0:
                    pool.wait_ge(s["const_in"], 7 * 16)
                pool.wait_ge(x_in[m.turn(RX)], m.round(RX, 16, 1))
                if m.base >= 4:
                    pool.wait_ge(s["finished"], m.lin(1, -3))
                pool.tensor_tensor(xo[:, m.turn(4)], x_sb[:, m.turn(RX)],
                                   offset_sb[:].unsqueeze(1).to_broadcast([P, SUB, D]), ALU.add).then_inc(s["xo_made"], 1)

            def gather(m):
                k, q = m.back(DENSE), m.turn(2)
                if m.base == DENSE:
                    pool.wait_ge(s["index_ready"], 1)
                pool.wait_ge(s["normed"], m.lin(1, -1))
                if m.base < DENSE + RX:
                    pool.wait_ge(s["xo_made"], m.lin(1, 1 - RX))
                else:
                    pool.wait_ge(s["edge_xo_made"], k.lin(1, 1 - RX))
                pool.tensor_copy(idx[:, q], index[:, 0:2, bass.ds(k.lin(SUB), SUB)]).then_inc(s["idx_ready"], 1)
                pool.wait_ge(s["idx_ready"], k.lin(1, 1))
                pool.sem_inc(s["pool_passed"], 1)
                for j in range(SUB):
                    for side, to in ((GATHER_SRC, x_sb[:, m.turn(RX), j]), (GATHER_DST, xd[:, q, j])):
                        pool.indirect_dma_start(to, None, x, bass.IndirectOffsetOnAxis(
                            ap=idx[:, q, side, j:j + 1], axis=0)).then_inc(gathered[q], 16)

            def scatter(m):
                k, q = m.back(DENSE), m.turn(2)
                if k.base >= 2:
                    pool.wait_ge(scat_out[q], k.round(2, 16 * SUB))
                pool.tensor_copy(idx_w[:, q], index[:, SCATTER, bass.ds(k.lin(SUB), SUB)]).then_inc(s["scat_idx_ready"], 1)
                pool.wait_ge(s["scat_idx_ready"], k.lin(1, 1))
                pool.wait_ge(s["finished"], m.lin(1, 1))
                pool.sem_inc(s["pool_passed"], 1)
                for j in range(SUB):
                    pool.indirect_dma_start(hidden, bass.IndirectOffsetOnAxis(ap=idx_w[:, q, j:j + 1], axis=0),
                                            fin[:, q, j], None, bounds_check=N - 1, oob_is_err=False).then_inc(scat_out[q], 16)

            def turn(runs, edge, sort):
                if runs(-3) and edge(-3):
                    gather(runs(-3))
                if runs(0) and not edge(0):
                    residual(runs(0))
                if runs(3) and edge(3):
                    if runs(3).base == DENSE:
                        pool.wait_ge(stored[0], DENSE_STORED)
                        pool.wait_ge(stored[1], DENSE_STORED)
                    scatter(runs(3))
                for name, do in (("hot", one_hots), ("move", move), ("reload", reload), ("attrs", sort_attrs)):
                    if sort(name):
                        do(*sort(name))
            pipeline(pool, turn, sort_steps=("hot", "move", "reload", "attrs"), **LAYER0)

            def gather_ahead(k):
                q = k.turn(2)
                if k.base >= 2:
                    pool.wait_ge(s["att_normed"], k.lin(1, -1))
                pool.tensor_copy(idx1[:, q], index[:, 0:2, bass.ds(k.lin(SUB), SUB)]).then_inc(s["att_idx_ready"], 1)
                pool.wait_ge(s["att_idx_ready"], k.lin(1, 1))
                pool.sem_inc(s["pool_passed"], 1)
                for j in range(SUB):
                    pool.indirect_dma_start(xd[:, q, j], None, hidden, bass.IndirectOffsetOnAxis(
                        ap=idx1[:, q, GATHER_DST, j:j + 1], axis=0)).then_inc(att_gathered[q], 16)

            def gather_own(k, j):
                q = k.turn(2)
                if k.base >= RX:
                    pool.wait_ge(s["att_added"], k.lin(SUB, SUB * (1 - RX) - SUB + 1 + j))
                    pool.sem_inc(s["pool_passed"], 1)
                pool.indirect_dma_start(x_sb[:, k.turn(RX), j], None, hidden, bass.IndirectOffsetOnAxis(
                    ap=idx1[:, q, GATHER_SRC, j:j + 1], axis=0)).then_inc(att_own[q], 16)

            def scatter_indices(k):
                q = k.turn(2)
                if k.base >= 2:
                    pool.wait_ge(att_out[q], k.round(2, 16 * SUB))
                pool.tensor_copy(idx_w[:, q], index[:, SCATTER, bass.ds(k.lin(SUB), SUB)]).then_inc(s["att_scat_ready"], 1)
                pool.wait_ge(s["att_scat_ready"], k.lin(1, 1))

            def scatter_out(k, j):
                q = k.turn(2)
                pool.wait_ge(s["att_added"], k.lin(SUB, j + 1))
                pool.sem_inc(s["pool_passed"], 1)
                pool.indirect_dma_start(out, bass.IndirectOffsetOnAxis(ap=idx_w[:, q, j:j + 1], axis=0),
                                        fin[:, q, j], None, bounds_check=N - 1, oob_is_err=False).then_inc(att_out[q], 16)

            for q in range(2):
                pool.wait_ge(scat_out[(DENSE + q) % 2], 16 * SUB * len(range(q, EDGE, 2)))

            def turn1(runs, edge):
                if runs(-3):
                    gather_ahead(runs(-3))
                if runs(1):
                    scatter_indices(runs(1))
                for j in range(SUB):
                    if runs(-3):
                        gather_own(runs(-3), j)
                    if runs(1):
                        scatter_out(runs(1), j)
            pipeline(pool, turn1, **LAYER1)
            for q in range(2):
                pool.wait_ge(att_out[q], 16 * SUB * len(range(q, EDGE, 2)))

        @block.vector
        def _(dve):
            for r, v in zip(raw[:4], (PAD_KEY, 0, 0, 0)):
                i = dve.memset(r[:], v)
            dve.memset(rec[:, :, 5:], 0)
            i.then_inc(s["raw_ready"], 1)
            dve.memset(ln_eps[:], LN_EPS)
            dve.memset(post_eps[:], POST_EPS)
            dve.memset(ones_f[:], 1.0)
            dve.memset(all_ones[:], 1.0)
            dve.memset(onehot[:, 0:2, :], 0.0)
            dve.wait_ge(s["iota_done"], 3)
            dve.tensor_copy(col_f[:], col_i[:]).then_inc(s["const_made"], 1)
            dve.tensor_copy(row_f[:], row_i[:]).then_inc(s["const_made"], 1)
            dve.wait_ge(s["const_made"], 2)
            dve.tensor_scalar(ident[:], col_f[:, 0:P], row_f[:, 0:1], None, ALU.is_equal)
            dve.tensor_scalar(before[:], col_f[:, 0:P], row_f[:, 0:1], None, ALU.is_gt)
            dve.tensor_scalar(not_before[:], col_f[:, 0:P], row_f[:, 0:1], None, ALU.is_le).then_inc(s["const_made"], 1)
            dve.wait_ge(s["edges_in"], 4 * 16)
            for c, r in enumerate(raw):
                i = dve.tensor_copy(rec[:, :, c], r[:])
            i.then_inc(s["rec_ready"], 1)
            def prepare_weights():
                dve.wait_ge(s["const_in"], 7 * 16)
                dve.tensor_scalar(self_w[:], eps_sb[:], 1.0, None, ALU.add).then_inc(s["self_w_ready"], 1)
                dve.memset(w_nat[:], 0.0).then_inc(s["w_filled"], 1)
                dve.memset(after[:], -1)
                dve.memset(prior[:], -1).then_inc(s["raw_ready"], 1)
                rest = b2_sb[:]
                dve.memset(b2_parts[:], 0.0)
                for part in range(3):
                    dve.tensor_copy(b2_bf[:, part], rest).then_inc(s["b2_step"], 1)
                    dve.wait_ge(s["b2_step"], 2 * part + 1)
                    if part < 2:
                        dve.tensor_tensor(b2_rest[:, part], rest, b2_bf[:, part], ALU.subtract).then_inc(s["b2_step"], 1)
                        dve.wait_ge(s["b2_step"], 2 * part + 2)
                        rest = b2_rest[:, part]
                for part in range(3):
                    one = slice(32 * part, 32 * part + 1)
                    last = dve.tensor_copy(b2_parts[one, :], b2_bf[one, part])
                last.then_inc(s["b2_ready"], 1)

            def digits(k, _):
                if k:
                    dve.wait_ge(s["sorted_in"], 16)
                else:
                    dve.wait_ge(s["rec_ready"], 1)
                dve.tensor_scalar(digit_i[:], rec[:, :, KEY], 8 * k, RADIX - 1, ALU.logical_shift_right,
                                  ALU.bitwise_and).then_inc(s["digit_ready"], 1)
                dve.wait_ge(s["digit_ready"], 2 * k + 1)
                dve.tensor_copy(digit_f[:], digit_i[:]).then_inc(s["digit_ready"], 1)
                dve.wait_ge(s["digit_ready"], 2 * k + 2)

            def one_hots(k, g):
                for u in range(HOT - HOT_POOL):
                    last = dve.tensor_scalar(onehot[:, bass.ds(g.lin(HOT, u + 2), 1), :].squeeze(1), col_f[:],
                                             digit_f[:, bass.ds(g.lin(HOT, u), 1)], None, ALU.is_equal)
                last.then_inc(s["onehot_ready"], 1)

            def bucket_starts(k, _):
                dve.wait_ge(s["counted"], (k + 1) * (T // HOT))
                dve.tensor_copy(counts[:], bank[6][:, 0:RADIX]).then_inc(s["bucket_step"], 1)
                dve.wait_ge(s["bucket_step"], 2 * k + 1)
                dve.tensor_tensor_scan(upto[:], ones_f[:], counts[:], 0.0, ALU.mult, ALU.add).then_inc(s["bucket_step"], 1)
                dve.wait_ge(s["bucket_step"], 2 * k + 2)
                dve.tensor_tensor(bucket[:], upto[:], counts[:], ALU.subtract).then_inc(s["bucket_ready"], 1)

            def read_ranks(k, g, pair):
                dve.wait_ge(s["rank_summed"], g.lin(2, 1 + pair + k * (T // 2)))
                for half in range(2):
                    u = 2 * pair + half
                    last = dve.scalar_tensor_tensor(
                        junk[:, half], bank[6 + half][:, 0:RADIX], 1.0, onehot[:, bass.ds(g.lin(SUB, 2 + u), 1), :].squeeze(1),
                        ALU.mult, ALU.mult, accum_out=place_f[:, g.turn(2), u:u + 1])
                last.then_inc(s["rank_read"], 1)

            def rows_of_places(k, g):
                b, before_ = g.turn(2), k * (T // SUB)
                dve.wait_ge(s["rank_read"], g.lin(2, 2 + k * (T // 2)))
                dve.tensor_copy(place_i[:, b], place_f[:, b]).then_inc(s["place_step"], 1)
                dve.wait_ge(s["place_step"], g.lin(2, 1 + 2 * before_))
                dve.tensor_scalar(place_lo[:, b], place_i[:, b], P - 1, None, ALU.bitwise_and)
                dve.tensor_scalar(place_hi[:, b], place_i[:, b], P.bit_length() - 1, None, ALU.logical_shift_right
                                  ).then_inc(s["place_step"], 1)
                if k or g.base >= 2:
                    dve.wait_ge(scattered[b], g.round(2, 16 * SUB, k * len(range(b, T // SUB, 2))))
                dve.wait_ge(s["place_step"], g.lin(2, 2 + 2 * before_))
                dve.scalar_tensor_tensor(place_row[:, b], place_lo[:, b], float(T), place_hi[:, b], ALU.mult,
                                         ALU.add).then_inc(s["place_ready"], 1)

            def fields(k, _):
                dve.wait_ge(s["sorted_in"], 5 * 16)
                dve.tensor_copy(key_f[:], rec[:, :, KEY])
                dve.tensor_copy(after_f[:], after[:, :, KEY])
                dve.tensor_copy(eid_f[:], rec[:, :, EID])
                dve.tensor_copy(prior_f[:], prior[:, :, KEY]).then_inc(s["fields_step"], 1)
                dve.wait_ge(s["fields_step"], 1)
                dve.tensor_tensor(same_next[:], key_f[:], after_f[:], ALU.is_equal)
                dve.tensor_tensor(same_prior[:], key_f[0:1], prior_f[:], ALU.is_equal)
                dve.tensor_scalar(index[:, GATHER_SRC], key_f[:], float(N - 1), None, ALU.min)
                dve.tensor_scalar(index[:, GATHER_EDGE], eid_f[:], float(E - 1), None, ALU.min)
                dve.tensor_copy(index[:, GATHER_DST], rec[:, :, DST])
                dve.tensor_scalar(w1_f[:], rec[:, :, WEIGHT1].bitcast(F32), float(HD) ** -0.5, None, ALU.mult
                                  ).then_inc(s["fields_step"], 1)
                dve.wait_ge(s["fields_step"], 2)
                dve.scalar_tensor_tensor(index[:, SCATTER], same_next[:], float(1 << 16), key_f[:], ALU.mult,
                                         ALU.add).then_inc(s["index_ready"], 1)

            def row_stats(m, edge, side):
                q, k = m.turn(2), m.back(DENSE)
                if side == 0:
                    if edge:
                        dve.wait_ge(gathered[q], k.round(2, 16 * 2 * SUB, 1))
                    else:
                        dve.wait_ge(x_in[m.turn(RX)], m.round(RX, 16, 1))
                of = xd[:, q] if side else x_sb[:, m.turn(RX)]
                for j in range(SUB):
                    last = dve.bn_stats(bn[:, side, j], of[:, j])
                if side == edge:
                    last.then_inc(s["stat_raw"], 1)

            def join_stats(m, edge):
                dve.wait_ge(s["stat_raw"], m.lin(1, 1))
                dve.sem_inc(s["dve_passed"], 1)
                for side in range(1 + edge):
                    for j in range(SUB):
                        last = dve.bn_aggr(mv[:, m.turn(2), side, j], bn[:, side, j])
                last.then_inc(s["stat"], 1)

            def inverse(m, edge):
                q, sides = m.turn(2), 1 + edge
                dve.wait_ge(s["std_ready"], m.lin(1, 1))
                dve.reciprocal(rstd[:, q, 0:sides], std[:, q, 0:sides]).then_inc(s["rstd_step"], 1)

            def shifts(m, edge):
                q, sides = m.turn(2), 1 + edge
                dve.wait_ge(s["rstd_step"], m.lin(1, 1))
                dve.scalar_tensor_tensor(shift[:, q, 0:sides], mv[:, q, 0:sides, :, 0], -1.0, rstd[:, q, 0:sides],
                                         ALU.mult, ALU.mult).then_inc(s["rstd_ready"], 1)

            def edge_residual(m):
                dve.wait_ge(s["finished"], m.lin(1, -3))
                dve.tensor_tensor(xo[:, m.turn(4)], x_sb[:, m.turn(RX)],
                                  offset_sb[:].unsqueeze(1).to_broadcast([P, SUB, D]), ALU.add).then_inc(s["edge_xo_made"], 1)

            def equality(m):
                k = m.back(DENSE)
                dve.wait_ge(s["key_turned"], k.lin(1, 1))
                dve.tensor_tensor(equal[:], bank[6][:].rearrange("p (j q) -> p j q", j=SUB),
                                  key_f[:, bass.ds(k.lin(SUB), SUB)].unsqueeze(2).to_broadcast([P, SUB, P]),
                                  ALU.is_equal).then_inc(s["equal_ready"], 1)

            def join_carry(m, j):
                k, row = m.back(DENSE), msg[0:1, m.turn(2), j]
                dve.wait_ge(s["weighted"], k.lin(1, 1))
                if j or k.base:
                    if j:
                        dve.wait_ge(s["summed"], k.lin(SUB, j))
                    else:
                        dve.wait_ge(s["carry_saved"], k.n)
                    before_ = bank[6 + (j - 1) % 2][0:1, D:2 * D] if j else carry_sb[:]
                    dve.scalar_tensor_tensor(row, before_, same_prior[:, bass.ds(k.lin(SUB, j), 1)], row,
                                             ALU.mult, ALU.add).then_inc(s["msg_ready"], 1)
                else:
                    dve.tensor_copy(row, row).then_inc(s["msg_ready"], 1)

            def own_and_sum(m, j):
                k, q = m.back(DENSE), m.turn(2)
                dve.wait_ge(s["summed"], k.lin(SUB, j + 1))
                if j == 0:
                    dve.wait_ge(s["normed"], m.lin(1, 1))
                    dve.wait_ge(s["turned"], m.lin(1, -1))
                dve.scalar_tensor_tensor(h[:, q, j], h_self[:, q, j], self_w[:, 0:1], bank[6 + j % 2][:, 0:D],
                                         ALU.mult, ALU.add).then_inc(s["block_h"], 1)

            def save_carry(m):
                dve.wait_ge(s["summed"], m.back(DENSE).lin(SUB, SUB))
                dve.tensor_copy(carry_sb[:], bank[7][0:1, D:2 * D]).then_inc(s["carry_saved"], 1)

            def out_stats(m):
                dve.wait_ge(s["relu_done"], m.lin(1, 1))
                for j in range(SUB):
                    last = dve.bn_stats(bn2[:, j], y[:, m.turn(2), j])
                last.then_inc(s["stat2_raw"], 1)

            def join_out_stats(m):
                dve.wait_ge(s["stat2_raw"], m.lin(1, 1))
                dve.sem_inc(s["dve_passed"], 1)
                for j in range(SUB):
                    last = dve.bn_aggr(mv2[:, m.turn(2), j], bn2[:, j])
                last.then_inc(s["stat2"], 1)

            def scale_out(m):
                q = m.turn(2)
                dve.wait_ge(s["stat2"], m.lin(1, 1))
                for j in range(SUB):
                    last = dve.scalar_tensor_tensor(y[:, q, j], y[:, q, j], mv2[:, q, j, 0:1], scale_sb[:], ALU.subtract, ALU.mult)
                last.then_inc(s["scaled"], 1)

            def out_inverse(m):
                dve.wait_ge(s["std2_ready"], m.lin(1, 1))
                dve.reciprocal(rstd2[:, m.turn(2)], std2[:, m.turn(2)]).then_inc(s["rstd2_ready"], 1)

            def finish(m):
                q = m.turn(2)
                if m.base >= DENSE + 2:
                    dve.wait_ge(scat_out[q], m.back(DENSE).round(2, 16 * SUB))
                elif m.base >= 2:
                    dve.wait_ge(stored[q], m.round(2, 32))
                if m.base >= DENSE:
                    dve.wait_ge(s["edge_xo_made"], m.back(DENSE).lin(1, 1))
                else:
                    dve.wait_ge(s["xo_made"], m.lin(1, 1))
                dve.wait_ge(s["scaled"], m.lin(1, 1))
                dve.wait_ge(s["rstd2_ready"], m.lin(1, 1))
                for j in range(SUB):
                    last = dve.scalar_tensor_tensor(fin[:, q, j], y[:, q, j], rstd2[:, q, j:j + 1], xo[:, m.turn(4), j],
                                                    ALU.mult, ALU.add)
                last.then_inc(s["finished"], 1)

            def turn(runs, edge, sort):
                m, f, g = runs(-2), runs(3), runs(-1) if edge(-1) else None
                if sort("hot"):
                    one_hots(*sort("hot"))
                if g:
                    equality(g)
                    join_carry(g, 0)
                if runs(0) and edge(0):
                    edge_residual(runs(0))
                if m:
                    row_stats(m, edge(-2), 0)
                if g:
                    join_carry(g, 1)
                    own_and_sum(g, 0)
                if m and edge(-2):
                    row_stats(m, True, 1)
                if g:
                    join_carry(g, 2)
                    own_and_sum(g, 1)
                if m and edge(-2):
                    join_stats(m, True)
                if f:
                    out_stats(f)
                if m and not edge(-2):
                    join_stats(m, False)
                if m and m.base == 0 and m.it is None:
                    prepare_weights()
                if m and edge(-2):
                    inverse(m, True)
                    shifts(m, True)
                if f:
                    join_out_stats(f)
                if sort("rank"):
                    read_ranks(*sort("rank"), pair=0)
                if m and not edge(-2):
                    inverse(m, False)
                    shifts(m, False)
                if f:
                    scale_out(f)
                    out_inverse(f)
                if g:
                    join_carry(g, 3)
                    own_and_sum(g, 2)
                if f:
                    finish(f)
                if g:
                    save_carry(g)
                    own_and_sum(g, 3)
                if sort("rank"):
                    read_ranks(*sort("rank"), pair=1)
                    rows_of_places(*sort("rank"))
                for name, do in (("digits", digits), ("bucket", bucket_starts), ("fields", fields)):
                    if sort(name):
                        do(*sort(name))
            pipeline(dve, turn, sort_steps=("digits", "hot", "bucket", "rank", "fields"), **LAYER0)

            def stats1(k, side):
                q = k.turn(2)
                if side:
                    dve.wait_ge(att_gathered[q], k.round(2, 16 * SUB, 1))
                else:
                    dve.wait_ge(att_own[q], k.round(2, 16 * SUB, 1))
                of = xd[:, q] if side else x_sb[:, k.turn(RX)]
                for j in range(SUB):
                    last = dve.bn_stats(bn[:, side, j], of[:, j])
                last.then_inc(s["att_stat_raw"], 1)

            def join_stats1(k):
                dve.wait_ge(s["att_stat_raw"], k.lin(2, 2))
                dve.sem_inc(s["dve_passed"], 1)
                for side in range(2):
                    for j in range(SUB):
                        last = dve.bn_aggr(mv[:, k.turn(2), side, j], bn[:, side, j])
                last.then_inc(s["att_stat"], 1)

            def inverse1(k):
                q = k.turn(2)
                dve.wait_ge(s["att_std_ready"], k.lin(1, 1))
                dve.reciprocal(rstd[:, q], std[:, q]).then_inc(s["att_rstd_step"], 1)

            def shifts1(k):
                q = k.turn(2)
                dve.wait_ge(s["att_rstd_step"], k.lin(1, 1))
                dve.scalar_tensor_tensor(shift[:, q], mv[:, q, :, :, 0], -1.0, rstd[:, q],
                                         ALU.mult, ALU.mult).then_inc(s["att_rstd_ready"], 1)

            def equality1(k):
                dve.wait_ge(s["att_key_turned"], k.lin(1, 1))
                dve.tensor_tensor(equal[:], bank[6][:].rearrange("p (j q) -> p j q", j=SUB),
                                  key_f[:, bass.ds(k.lin(SUB), SUB)].unsqueeze(2).to_broadcast([P, SUB, P]),
                                  ALU.is_equal).then_inc(s["att_equal_ready"], 1)

            def products(k, pair):
                tiles = (2 * pair, 2 * pair + 1)
                if pair == 0:
                    dve.wait_ge(attr_in[k.turn(RX)], k.round(RX, 16, 1))
                for j in tiles:
                    dve.wait_ge(s["att_qkv_done"], k.lin(SUB, j + 1))
                    dve.tensor_tensor(prod[:, j % 2], bank[2 + 2 * (j % 2)][:, 0:D], xo[:, k.turn(RX), j], ALU.mult
                                      ).then_inc(s["att_qw"], 1)
                for j in tiles:
                    dve.wait_ge(s["att_qw"], k.lin(SUB, j + 1))
                    half = prod[:, j % 2].rearrange("p (c f) -> p c f", c=CH)
                    dve.tensor_tensor(half, half, kv_bank(j)[:, :, 0], ALU.mult).then_inc(s["att_qwk"], 1)

            def attend(k, pair):
                tiles = (2 * pair, 2 * pair + 1)
                for j in tiles:
                    dve.wait_ge(s["att_qwk"], k.lin(SUB, j + 1))
                    dve.tensor_reduce(alpha[:, j % 2], prod[:, j % 2].rearrange("p (h f) -> p h f", h=H),
                                      mybir.AxisListType.X, ALU.add).then_inc(s["att_alpha"], 1)
                for j in tiles:
                    dve.wait_ge(s["att_alpha"], k.lin(SUB, j + 1))
                    if j >= 2 or k.base:
                        dve.wait_ge(s["att_msg"], k.lin(SUB, j - 1))
                    dve.tensor_scalar(alpha_w[:, j % 2], alpha[:, j % 2], w1_f[:, bass.ds(k.lin(SUB, j), 1)], None,
                                      ALU.mult).then_inc(s["att_alpha_w"], 1)

            def join_carry1(k, j):
                q = k.turn(2)
                row = msg[0:1, q, j]
                dve.wait_ge(s["att_msg"], k.lin(SUB, j + 1))
                if j or k.base:
                    if j:
                        dve.wait_ge(s["att_summed"], k.lin(SUB, j))
                    else:
                        dve.wait_ge(s["att_carry_saved"], k.n)
                    before_ = bank[6 + (j - 1) % 2][0:1, D:2 * D] if j else carry_sb[:]
                    dve.scalar_tensor_tensor(row, before_, same_prior[:, bass.ds(k.lin(SUB, j), 1)], row,
                                             ALU.mult, ALU.add).then_inc(s["att_msg_ready"], 1)
                else:
                    dve.tensor_copy(row, row).then_inc(s["att_msg_ready"], 1)

            def total(k, j):
                q = k.turn(2)
                dve.wait_ge(s["att_summed"], k.lin(SUB, j + 1))
                if j == 0 and k.base >= 2:
                    dve.wait_ge(att_out[q], k.round(2, 16 * SUB))
                last = dve.tensor_tensor(fin[:, q, j], bank[6 + j % 2][:, 0:D], x_sb[:, k.turn(RX), j], ALU.add)
                last.then_inc(s["att_added"], 1)

            def save_carry1(k):
                dve.wait_ge(s["att_summed"], k.lin(SUB, SUB))
                dve.tensor_copy(carry_sb[:], bank[7][0:1, D:2 * D]).then_inc(s["att_carry_saved"], 1)

            def turn1(runs, edge):
                m, k, g = runs(-2), runs(0), runs(1)
                if g:
                    equality1(g)
                    join_carry1(g, 0)
                if k:
                    products(k, 0)
                if g:
                    join_carry1(g, 1)
                if k:
                    attend(k, 0)
                if g:
                    total(g, 0)
                if m:
                    stats1(m, 1)
                if g:
                    join_carry1(g, 2)
                    total(g, 1)
                if m:
                    stats1(m, 0)
                if k:
                    products(k, 1)
                if g:
                    join_carry1(g, 3)
                if k:
                    attend(k, 1)
                if m:
                    join_stats1(m)
                if g:
                    total(g, 2)
                    save_carry1(g)
                    total(g, 3)
                if m:
                    inverse1(m)
                    shifts1(m)
            pipeline(dve, turn1, **LAYER1)


        @block.scalar
        def _(act):
            def deviation(m, edge):
                q, sides = m.turn(2), 1 + edge
                act.wait_ge(s["stat"], m.lin(1, 1))
                act.activation(std[:, q, 0:sides], mv[:, q, 0:sides, :, 1], ACT.Sqrt, bias=ln_eps[:, 0:1]).then_inc(s["std_ready"], 1)

            def normalise(m, edge):
                q = m.turn(2)
                act.wait_ge(s["rstd_ready"], m.lin(1, 1))
                if edge:
                    if m.base >= DENSE + 2:
                        act.wait_ge(s["block_h"], m.back(DENSE).lin(SUB, -SUB))
                    to = h_self[:, q]
                else:
                    if m.base >= 2:
                        act.wait_ge(s["turned"], m.lin(1, -1))
                    to = h[:, q]
                for j in range(SUB):
                    last = act.activation(to[:, j], x_sb[:, m.turn(RX), j], ACT.Relu, bias=shift[:, q, 0, j:j + 1],
                                          scale=rstd[:, q, 0, j:j + 1])
                last.then_inc(s["normed"], 1)

            def normalise_other(m):
                q = m.turn(2)
                act.wait_ge(s["rstd_ready"], m.lin(1, 1))
                if m.base >= DENSE + 2:
                    act.wait_ge(s["summed"], m.back(DENSE).lin(SUB, -SUB))
                for j in range(SUB):
                    last = act.activation(msg[:, q, j], xd[:, q, j], ACT.Relu, bias=shift[:, q, 1, j:j + 1],
                                          scale=rstd[:, q, 1, j:j + 1])
                last.then_inc(s["other_normed"], 1)

            def spread_keys(m):
                k = m.back(DENSE)
                if k.base:
                    act.wait_ge(s["key_turned"], k.n)
                act.activation(key_b[:], key_f[:, bass.ds(k.lin(SUB), SUB)].unsqueeze(2).to_broadcast([P, SUB, P]),
                               ACT.Copy).then_inc(s["key_spread"], 1)

            def weigh(m):
                k, q = m.back(DENSE), m.turn(2)
                act.wait_ge(s["other_normed"], k.lin(1, 1))
                for j in range(SUB):
                    last = act.activation(msg[:, q, j], msg[:, q, j], ACT.Copy,
                                          scale=rec[:, bass.ds(k.lin(SUB, j), 1), WEIGHT0].bitcast(F32))
                last.then_inc(s["weighted"], 1)

            def take_hT(m, edge):
                if m.base == 0:
                    act.wait_ge(s["self_w_ready"], 1)
                scale = 1.0 if edge else self_w[:, 0:1]
                act.wait_ge(s["turned"], m.lin(1, 1))
                if m.base >= 2:
                    act.wait_ge(s["l1_done"], m.lin(1, -1))
                for c in range(CH):
                    last = act.activation(hT[:, m.turn(2), c], bank[c][:], ACT.Copy, scale=scale)
                last.then_inc(s["hT_ready"], 1)

            def take_z1(m):
                act.wait_ge(s["l1_done"], m.lin(1, 1))
                if m.base >= 2:
                    act.wait_ge(s["l2_done"], m.lin(1, -1))
                for c in range(CH):
                    last = act.activation(z1[:, m.turn(2), c], bank[2 + c][:], ACT.Relu, bias=b1_sb[:, c:c + 1])
                last.then_inc(s["z1_ready"], 1)

            def relu(m):
                act.wait_ge(s["l2_done"], m.lin(1, 1))
                if m.base >= 2:
                    act.wait_ge(s["finished"], m.lin(1, -1))
                for c in range(2):
                    last = act.activation(y[:, m.turn(2), 2 * c:2 * c + 2], bank[4 + c][:].rearrange("p (j f) -> p j f", j=2),
                                          ACT.Relu)
                last.then_inc(s["relu_done"], 1)

            def deviation2(m):
                act.wait_ge(s["stat2"], m.lin(1, 1))
                act.activation(std2[:, m.turn(2)], mv2[:, m.turn(2), :, 1], ACT.Sqrt, bias=post_eps[:, 0:1]).then_inc(s["std2_ready"], 1)

            def store_attrs(_, g):
                b = g.turn(2)
                act.wait_ge(attr_got[b], g.round(2, 16 * SUB, 1))
                act.dma_start(block_rows(attr_sorted, g), attr_sb[:, b]).then_inc(attr_stored[b], 16)

            def turn(runs, edge, sort):
                if runs(3):
                    relu(runs(3))
                if runs(-2) and edge(-2):
                    if runs(-2).base == DENSE:
                        act.wait_ge(s["index_ready"], 1)
                    spread_keys(runs(-2))
                if runs(0):
                    take_hT(runs(0), edge(0))
                if runs(-2):
                    deviation(runs(-2), edge(-2))
                if runs(3) and not edge(-2):
                    deviation2(runs(3))
                if runs(1):
                    take_z1(runs(1))
                if runs(3) and edge(-2):
                    deviation2(runs(3))
                if runs(-2):
                    if edge(-2):
                        normalise_other(runs(-2))
                        weigh(runs(-2))
                    normalise(runs(-2), edge(-2))
                if sort("attrs_out"):
                    store_attrs(*sort("attrs_out"))
            act.wait_ge(s["const_in"], 7 * 16)
            pipeline(act, turn, sort_steps=("attrs_out",), **LAYER0)

            act.wait_ge(s["w_ready"], 1)
            for c in range(CH):
                last = act.activation(w_qkv[:, c], bank[6 + c][:, 0:3 * P], ACT.Copy)
            last.then_inc(s["w_taken"], 1)

            def deviation1(k):
                q = k.turn(2)
                act.wait_ge(s["att_stat"], k.lin(1, 1))
                act.activation(std[:, q], mv[:, q, :, :, 1], ACT.Sqrt, bias=ln_eps[:, 0:1]).then_inc(s["att_std_ready"], 1)

            def message(k, pair):
                for j in (2 * pair, 2 * pair + 1):
                    act.wait_ge(s["att_alpha_w"], k.lin(SUB, j + 1))
                    if j == 0 and k.base >= 2:
                        act.wait_ge(s["att_summed"], k.lin(SUB, -SUB))
                    for hh in range(H):
                        c, o = hh // 2, hh % 2 * HD
                        last = act.activation(msg[:, k.turn(2), j, hh * HD:(hh + 1) * HD], kv_bank(j)[:, c, 1, o:o + HD],
                                              ACT.Copy, scale=alpha_w[:, j % 2, hh:hh + 1])
                    last.then_inc(s["att_msg"], 1)

            def normalise1(k):
                q = k.turn(2)
                act.wait_ge(s["att_rstd_ready"], k.lin(1, 1))
                if k.base >= 2:
                    act.wait_ge(s["att_turned"], k.lin(2, -2))
                for side, (of, to) in enumerate(((x_sb[:, k.turn(RX)], h[:, q]), (xd[:, q], y[:, q]))):
                    for j in range(SUB):
                        last = act.activation(to[:, j], of[:, j], ACT.Relu, bias=shift[:, q, side, j:j + 1],
                                              scale=rstd[:, q, side, j:j + 1])
                last.then_inc(s["att_normed"], 1)

            def spread_keys1(k):
                if k.base:
                    act.wait_ge(s["att_key_turned"], k.n)
                act.activation(key_b[:], key_f[:, bass.ds(k.lin(SUB), SUB)].unsqueeze(2).to_broadcast([P, SUB, P]),
                               ACT.Copy).then_inc(s["att_key_spread"], 1)

            def take_turned1(k, side):
                act.wait_ge(s["att_turned"], k.lin(2, side + 1))
                if k.base >= 2:
                    act.wait_ge(s["att_qkv_done"], k.lin(SUB, -SUB))
                for c in range(CH):
                    last = act.activation((hT, z1)[side][:, k.turn(2), c], bank[c][:], ACT.Copy)
                last.then_inc(s["att_turned_taken"], 1)

            def turn1(runs, edge):
                if runs(0):
                    message(runs(0), 0)
                    spread_keys1(runs(0))
                if runs(-1):
                    take_turned1(runs(-1), 0)
                if runs(-1):
                    take_turned1(runs(-1), 1)
                if runs(0):
                    message(runs(0), 1)
                if runs(-2):
                    deviation1(runs(-2))
                if runs(-2):
                    normalise1(runs(-2))
            pipeline(act, turn1, **LAYER1)


        @block.tensor
        def _(pe):
            pe.wait_ge(s["const_made"], 3)

            def count(k, g):
                pe.wait_ge(s["onehot_ready"], g.lin(1, 1 + k * (T // HOT)))
                pe.wait_ge(s["onehot_ready_pool"], g.lin(1, 1 + k * (T // HOT)))
                first = g.it is None and g.base == 0
                for u in range(HOT):
                    mm = pe.matmul(bank[6][:, 0:RADIX], all_ones[:], onehot[:, bass.ds(g.lin(HOT, 2 + u), 1), :].squeeze(1),
                                   start=first and u == 0, stop=True, skip_group_check=True)
                mm.then_inc(s["counted"], 1)

            def start_ranks(k, _):
                pe.wait_ge(s["bucket_ready"], k + 1)
                for half in range(2):
                    pe.matmul(bank[6 + half][:, 0:RADIX], ident[:], bucket[:], start=True, stop=True)

            def rank_pair(k, g, pair):
                if k or g.base or pair:
                    pe.wait_ge(s["rank_read"], g.lin(2, pair + k * (T // 2)))
                for half in range(2):
                    for add, lhs in enumerate((not_before, all_ones, before)):
                        mm = pe.matmul(bank[6 + half][:, 0:RADIX], lhs[:],
                                       onehot[:, bass.ds(g.lin(SUB, 2 * pair + half + add), 1), :].squeeze(1), start=False,
                                       stop=True, skip_group_check=True)
                mm.then_inc(s["rank_summed"], 1)

            def turn_h(m):
                q = m.turn(2)
                if m.base >= DENSE:
                    pe.wait_ge(s["block_h"], m.back(DENSE).lin(SUB, SUB))
                else:
                    pe.wait_ge(s["normed"], m.lin(1, 1))
                if m.base:
                    pe.wait_ge(s["hT_ready"], m.n)
                for c in range(CH):
                    for j in range(SUB):
                        mm = pe.transpose(bank[c][:, j * P:(j + 1) * P], h[:, q, j, c * P:(c + 1) * P], ident[:])
                mm.then_inc(s["turned"], 1)

            def layer1(m, o):
                if o == 0:
                    pe.wait_ge(s["hT_ready"], m.lin(1, 1))
                    if m.base:
                        pe.wait_ge(s["z1_ready"], m.n)
                for c in range(CH):
                    mm = pe.matmul(bank[2 + o][:], W1_sb[:, c, o * P:(o + 1) * P], hT[:, m.turn(2), c],
                                   start=(c == 0), stop=(c == CH - 1))
                if o == CH - 1:
                    mm.then_inc(s["l1_done"], 1)

            def layer2(m, half):
                if half == 0:
                    pe.wait_ge(s["z1_ready"], m.lin(1, 1))
                    if m.base:
                        pe.wait_ge(s["relu_done"], m.n)
                for j in (2 * half, 2 * half + 1):
                    to = bank[4 + half][:, j % 2 * D:(j % 2 + 1) * D]
                    pe.matmul(to, all_ones[:], b2_parts[:], start=True, stop=False)
                    for c in range(CH):
                        mm = pe.matmul(to, z1[:, m.turn(2), c, j * P:(j + 1) * P], W2_sb[:, c], start=False,
                                       stop=(c == CH - 1))
                if half:
                    mm.then_inc(s["l2_done"], 1)

            def turn_keys(m):
                k = m.back(DENSE)
                pe.wait_ge(s["key_spread"], k.lin(1, 1))
                if k.base:
                    pe.wait_ge(s["block_h"], k.lin(SUB, -1))
                for j in range(SUB):
                    mm = pe.transpose(bank[6][:, j * P:(j + 1) * P], key_b[:, j], ident[:])
                mm.then_inc(s["key_turned"], 1)

            def sums(m, j):
                k, q = m.back(DENSE), m.turn(2)
                if j == 0:
                    pe.wait_ge(s["equal_ready"], k.lin(1, 1))
                pe.wait_ge(s["msg_ready"], k.lin(SUB, j + 1))
                if j >= 2 or k.base:
                    pe.wait_ge(s["block_h"], k.lin(SUB, j - 1))
                pe.matmul(bank[6 + j % 2][0:1, D:2 * D], equal[:, j, P - 1:P], msg[:, q, j], start=True, stop=True)
                pe.matmul(bank[6 + j % 2][:, 0:D], equal[:, j], msg[:, q, j], start=True, stop=True).then_inc(s["summed"], 1)

            def turn(runs, edge, sort):
                g = runs(-1) if edge(-1) else None
                if sort("rank") and sort("rank")[1].base == 0 and sort("rank")[1].it is None:
                    start_ranks(*sort("rank"))
                if runs(1):
                    layer1(runs(1), 0)
                if runs(0):
                    turn_h(runs(0))
                if sort("rank"):
                    rank_pair(*sort("rank"), pair=0)
                if g:
                    sums(g, 0)
                if runs(1):
                    layer1(runs(1), 1)
                if g:
                    sums(g, 1)
                if runs(2):
                    layer2(runs(2), 0)
                if sort("rank"):
                    rank_pair(*sort("rank"), pair=1)
                if g:
                    sums(g, 2)
                if runs(2):
                    layer2(runs(2), 1)
                if g:
                    sums(g, 3)
                if runs(-2) and edge(-2):
                    turn_keys(runs(-2))
                if sort("hot"):
                    count(*sort("hot"))
            pe.wait_ge(s["b2_ready"], 1)
            pipeline(pe, turn, sort_steps=("hot", "rank"), **LAYER0)

            pe.wait_ge(s["block_h"], EDGE * SUB)
            pe.wait_ge(s["carry_saved"], EDGE)
            pe.wait_ge(s["w_in"], 16 * 3 * H)
            for k in range(3):
                for c in range(CH):
                    mm = pe.transpose(bank[6 + c][:, k * P:(k + 1) * P], w_nat[:, k, c], ident[:])
            mm.then_inc(s["w_ready"], 1)
            pe.wait_ge(s["w_taken"], 1)


            def turn1_rows(k, side):
                q = k.turn(2)
                pe.wait_ge(s["att_normed"], k.lin(1, 1))
                if side or k.base:
                    pe.wait_ge(s["att_turned_taken"], k.lin(2, side))
                for c in range(CH):
                    for j in range(SUB):
                        mm = pe.transpose(bank[c][:, j * P:(j + 1) * P], (h, y)[side][:, q, j, c * P:(c + 1) * P], ident[:])
                mm.then_inc(s["att_turned"], 1)

            def turn_keys1(k):
                pe.wait_ge(s["att_key_spread"], k.lin(1, 1))
                if k.base:
                    pe.wait_ge(s["att_added"], k.lin(SUB, -1))
                for j in range(SUB):
                    mm = pe.transpose(bank[6][:, j * P:(j + 1) * P], key_b[:, j], ident[:])
                mm.then_inc(s["att_key_turned"], 1)

            def qkv(k, j):
                q = k.turn(2)
                if j == 0:
                    pe.wait_ge(s["att_turned_taken"], k.lin(2, 2))
                if j >= 2 or k.base:
                    pe.wait_ge(s["att_msg"], k.lin(SUB, j - 1))
                for c in range(CH):
                    pe.matmul(bank[2 + 2 * (j % 2)][:, c * P:(c + 1) * P], hT[:, q, c, j * P:(j + 1) * P], w_qkv[:, c, 0],
                              start=True, stop=True)
                    mm = pe.matmul(bank[3 + 2 * (j % 2)][:, c * D:(c + 1) * D], z1[:, q, c, j * P:(j + 1) * P],
                                   w_qkv[:, c, 1:3], start=True, stop=True)
                mm.then_inc(s["att_qkv_done"], 1)

            def sums1(k, j):
                q = k.turn(2)
                if j == 0:
                    pe.wait_ge(s["att_equal_ready"], k.lin(1, 1))
                pe.wait_ge(s["att_msg_ready"], k.lin(SUB, j + 1))
                if j >= 2 or k.base:
                    pe.wait_ge(s["att_added"], k.lin(SUB, j - 1))
                pe.matmul(bank[6 + j % 2][0:1, D:2 * D], equal[:, j, P - 1:P], msg[:, q, j], start=True, stop=True)
                pe.matmul(bank[6 + j % 2][:, 0:D], equal[:, j], msg[:, q, j], start=True, stop=True).then_inc(s["att_summed"], 1)

            def turn1(runs, edge):
                ahead, k, g = runs(-1), runs(0), runs(1)
                if g:
                    sums1(g, 0)
                    sums1(g, 1)
                if ahead:
                    turn1_rows(ahead, 0)
                if k:
                    qkv(k, 2)
                    qkv(k, 3)
                if g:
                    sums1(g, 2)
                if ahead:
                    turn1_rows(ahead, 1)
                if g:
                    sums1(g, 3)
                if k:
                    turn_keys1(k)
                if ahead:
                    qkv(ahead, 0)
                    qkv(ahead, 1)
            pipeline(pe, turn1, **LAYER1)



def kernel(**inputs):
    import numpy as np
    import concourse.bacc as bacc
    from concourse.bass_utils import run_bass_kernel_spmd

    names = ["x", "src", "dst", "edge_attr_256", "edge_weight", "edge_weight1", "L0_gnn_W1", "L0_gnn_b1", "L0_gnn_W2",
             "L0_gnn_b2", "L0_gnn_eps", "L0_gnn_offset", "L0_gnn_scale", "L1_gnn_Wq", "L1_gnn_Wk", "L1_gnn_Wv"]
    nc = bacc.Bacc("TRN2", target_bir_lowering=False, num_devices=1)
    arrays, args = {}, []
    for name in names:
        a = np.ascontiguousarray(inputs[name])
        arrays[f"in_{name}"] = a
        args.append(nc.dram_tensor(f"in_{name}", a.shape, mybir.dt.from_np(a.dtype), kind="ExternalInput").ap())
    shape = inputs["x"].shape
    args.append(nc.dram_tensor("result", shape, F32, kind="ExternalOutput").ap())
    gnn_kernel(nc, *args)
    r = run_bass_kernel_spmd(nc, [arrays], core_ids=[0])
    return r.results[0]["result"]
```
